# Optimizing a Trainium2 kernel written in Bass

```python
import numpy as np
import jax
import jax.numpy as jnp

def _softmax(x, axis=-1):
    return jax.nn.softmax(x, axis=axis)
def _gelu(x):
    return jax.nn.gelu(x, approximate=True)
def _silu(x):
    return jax.nn.silu(x)
def _sigmoid(x):
    return jax.nn.sigmoid(x)
def _layernorm(x, axis=-1, eps=1e-5):
    m = jnp.mean(x, axis=axis, keepdims=True)
    v = jnp.var(x, axis=axis, keepdims=True)
    return (x - m) / jnp.sqrt(v + eps)
def _scatter_add(tgt, idx, src, axis=0):
    return tgt.at[idx].add(src)
def _segment_sum(src, seg, n):
    return jax.ops.segment_sum(src, seg, n)

kernel_name = 'mk_conv_preact_d1_conv_nhwc512_f459be'

def setup_inputs(seed: int = 0):
    np.random.seed(seed)
    _w = jnp.asarray
    def _rec_inputs():
        import jax
        import jax.numpy as jnp
        _gk = jax.random.key(seed)
        x = -0.000125 + 0.9999 * jax.random.normal(jax.random.fold_in(_gk, 1), (16, 64, 64, 512), jnp.float32)
        return x
    x = _rec_inputs()
    def _L0_conv_setup():
        import jax, jax.numpy as jnp
        import numpy as np
        B, H, W, C = (16, 64, 64, 512)
        C2 = C // 2
        LN_EPS = 0.001
        key = jax.random.key(seed)
        ks = jax.random.split(key, 8)
        s = 0.02
        return {'x': jax.random.normal(ks[0], (B, H, W, C), dtype=jnp.float32), 'ch_wv_w': jax.random.normal(ks[1], (C, C2), dtype=jnp.float32) * s, 'ch_wv_b': jnp.zeros((C2,), jnp.float32), 'ch_wq_w': jax.random.normal(ks[2], (C, 1), dtype=jnp.float32) * s, 'ch_wq_b': jnp.zeros((1,), jnp.float32), 'ch_wz_w': jax.random.normal(ks[3], (C2, C), dtype=jnp.float32) * s, 'ch_wz_b': jnp.zeros((C,), jnp.float32), 'ln_gamma': jnp.ones((C,), jnp.float32), 'ln_beta': jnp.zeros((C,), jnp.float32), 'sp_wv_w': jax.random.normal(ks[4], (C, C2), dtype=jnp.float32) * s, 'sp_wv_b': jnp.zeros((C2,), jnp.float32), 'sp_wq_w': jax.random.normal(ks[5], (C, C2), dtype=jnp.float32) * s, 'sp_wq_b': jnp.zeros((C2,), jnp.float32)}
    _L0_conv_all = _L0_conv_setup()
    _L0_conv_in = {k: v for k, v in _L0_conv_all.items() if k in ('ch_wv_w', 'ch_wv_b', 'ch_wq_w', 'ch_wq_b', 'ch_wz_w', 'ch_wz_b', 'ln_gamma', 'ln_beta', 'sp_wv_w', 'sp_wv_b', 'sp_wq_w', 'sp_wq_b', )}
    del _L0_conv_all

    return {
        "x": x,
        "L0_conv_ch_wv_w": _L0_conv_in["ch_wv_w"],
        "L0_conv_ch_wv_b": _L0_conv_in["ch_wv_b"],
        "L0_conv_ch_wq_w": _L0_conv_in["ch_wq_w"],
        "L0_conv_ch_wq_b": _L0_conv_in["ch_wq_b"],
        "L0_conv_ch_wz_w": _L0_conv_in["ch_wz_w"],
        "L0_conv_ch_wz_b": _L0_conv_in["ch_wz_b"],
        "L0_conv_ln_gamma": _L0_conv_in["ln_gamma"],
        "L0_conv_ln_beta": _L0_conv_in["ln_beta"],
        "L0_conv_sp_wv_w": _L0_conv_in["sp_wv_w"],
        "L0_conv_sp_wv_b": _L0_conv_in["sp_wv_b"],
        "L0_conv_sp_wq_w": _L0_conv_in["sp_wq_w"],
        "L0_conv_sp_wq_b": _L0_conv_in["sp_wq_b"],
    }

def reference(x, L0_conv_ch_wv_w, L0_conv_ch_wv_b, L0_conv_ch_wq_w, L0_conv_ch_wq_b, L0_conv_ch_wz_w, L0_conv_ch_wz_b, L0_conv_ln_gamma, L0_conv_ln_beta, L0_conv_sp_wv_w, L0_conv_sp_wv_b, L0_conv_sp_wq_w, L0_conv_sp_wq_b):
    import jax
    import jax.numpy as jnp
    def _L0_conv_ref(x, ch_wv_w, ch_wv_b, ch_wq_w, ch_wq_b, ch_wz_w, ch_wz_b, ln_gamma, ln_beta, sp_wv_w, sp_wv_b, sp_wq_w, sp_wq_b):
        import jax, jax.numpy as jnp
        import numpy as np
        B, H, W, C = (16, 64, 64, 512)
        C2 = C // 2
        LN_EPS = 0.001
        b, h, w, c = x.shape
        n = h * w
        c2 = c // 2
        ch_wv = jnp.einsum('bhwc,cd->bhwd', x, ch_wv_w) + ch_wv_b
        ch_wq = jnp.einsum('bhwc,co->bhwo', x, ch_wq_w) + ch_wq_b
        ch_wv = ch_wv.reshape(b, n, c2)
        ch_wq = jax.nn.softmax(ch_wq.reshape(b, n, 1), axis=1)
        ch_wz = jnp.einsum('bnd,bno->bd', ch_wv, ch_wq)
        ch_wz = jnp.einsum('bd,dc->bc', ch_wz, ch_wz_w) + ch_wz_b
        mean = jnp.mean(ch_wz, axis=-1, keepdims=True)
        var = jnp.var(ch_wz, axis=-1, keepdims=True)
        ch_wz = (ch_wz - mean) * jax.lax.rsqrt(var + LN_EPS) * ln_gamma + ln_beta
        channel_weight = jax.nn.sigmoid(ch_wz)[:, None, None, :]
        channel_out = channel_weight * x
        sp_wv = jnp.einsum('bhwc,cd->bhwd', channel_out, sp_wv_w) + sp_wv_b
        sp_wq = jnp.einsum('bhwc,cd->bhwd', channel_out, sp_wq_w) + sp_wq_b
        sp_wq = jnp.mean(sp_wq, axis=(1, 2))
        sp_wq = jax.nn.softmax(sp_wq, axis=-1)
        sp_wv = sp_wv.reshape(b, n, c2)
        sp_wz = jnp.einsum('bd,bnd->bn', sp_wq, sp_wv)
        spatial_weight = jax.nn.sigmoid(sp_wz).reshape(b, h, w, 1)
        return spatial_weight * channel_out

    def _gn(v, G=32, eps=1e-5):
        B_, H_, W_, C_ = v.shape
        g = v.reshape(B_, H_, W_, G, C_ // G)
        m = jnp.mean(g, axis=(1, 2, 4), keepdims=True)
        s = jnp.var(g, axis=(1, 2, 4), keepdims=True)
        return ((g - m) / jnp.sqrt(s + eps)).reshape(v.shape)

    def _ln_c(v, eps=1e-6):
        m = jnp.mean(v, axis=-1, keepdims=True)
        s = jnp.var(v, axis=-1, keepdims=True)
        return (v - m) / jnp.sqrt(s + eps)

    def _ln_t(v, eps=1e-5):
        m = jnp.mean(v, axis=-1, keepdims=True)
        s = jnp.var(v, axis=-1, keepdims=True)
        return (v - m) / jnp.sqrt(s + eps)

    def _to_tokens(v):
        B_, H_, W_, C_ = v.shape
        return v.reshape(B_, H_ * W_, C_)
    def _from_tokens(t, like):
        return t.reshape(like.shape)

    x = x + _L0_conv_ref(_gn(x), L0_conv_ch_wv_w, L0_conv_ch_wv_b, L0_conv_ch_wq_w, L0_conv_ch_wq_b, L0_conv_ch_wz_w, L0_conv_ch_wz_b, L0_conv_ln_gamma, L0_conv_ln_beta, L0_conv_sp_wv_w, L0_conv_sp_wv_b, L0_conv_sp_wq_w, L0_conv_sp_wq_b)
    return x


_drawn_inputs = setup_inputs


def setup_inputs(seed=0):
    import zlib

    import numpy as np

    out = dict(_drawn_inputs(seed))
    spreads = {'L0_conv_ch_wv_b': (0.0, 1.134),
     'L0_conv_ch_wz_b': (0.0, 0.345),
     'L0_conv_ln_gamma': (1.0, 0.6),
     'L0_conv_ln_beta': (0.0, 0.8),
     'L0_conv_sp_wv_b': (0.0, 2.0),
     'L0_conv_sp_wq_b': (0.0, 2.0)}
    factors = {'L0_conv_ch_wv_w': 8.0,
     'L0_conv_ch_wq_w': 8.0,
     'L0_conv_sp_wv_w': 25.089,
     'L0_conv_sp_wq_w': 64.0}
    for name, (base, spread) in spreads.items():
        noise = np.random.default_rng([zlib.crc32(name.encode()), seed]).standard_normal(out[name].shape)
        drawn = base * np.exp(spread * noise) if base else spread * noise
        out[name] = jnp.asarray(drawn.astype(out[name].dtype))
    for name, factor in factors.items():
        out[name] = (out[name] * factor).astype(out[name].dtype)
    return out
```

```python
from contextlib import ExitStack

import concourse.bass as bass
from concourse import mybir

F32 = mybir.dt.float32
BF16 = mybir.dt.bfloat16
ALU = mybir.AluOpType
ACT = mybir.ActivationFunctionType
AX = mybir.AxisListType

P = 128
IMAGES, TOKENS, C = 16, 64 * 64, 512
TILES = TOKENS // P
J = C // P
D = C // 2
H = D // P
GROUP = 16
CHUNK = 8
CHUNKS = TILES // CHUNK
STRIPS = 4
SW = P // STRIPS
PAIR = 2
GN_EPS, LN_EPS = 1e-5, 1e-3

EVENTS = (
    "sum_copied", "square_col", "stat_ps", "stat_mean", "stat_group_ps", "stat_group", "stat_group_sb", "stat_m2", "stat_var",
    "rs", "wq_col", "mwq_col", "wq_diag", "wq_row",
    "logits_max", "max_t", "max_one", "max_ps", "max_neg", "probs",
    "weighted_ps", "mass_ps", "weighted", "mass_inv", "pooled_ps", "pooled_n", "pooled",
    "v_ps", "v", "z_ps", "z", "z_mean_ps", "z_mean", "z_cent", "z_sq", "z_var_ps", "z_var", "z_rstd",
    "z_norm", "z_gamma", "z_beta", "z_exp", "z_den", "cw", "u", "w", "y_cent", "y_mean",
    "q_ps", "q_row", "q_max", "q_exp", "q_inv", "a_ps", "a", "k_ps", "v_col",
    "shift_a", "shift_b", "shift_ps", "shift", "v_diag", "v_row", "u_diag", "u_ps", "u_row", "w_diag", "w_ps",
    "w_row",
)


class Image:

    def __init__(self, b, slot, use):
        self.b, self.slot, self.use = b, slot, use

    def at(self, count, n):
        return self.b * count + n


def comes(value):
    return not isinstance(value, int) or value > 0


def image(i, off):
    return Image(i * 2 + off, off % 2, i + off // 2)


def build(nc, x, w, out):
    ctx = ExitStack()
    with ctx:
        def sb(name, shape, dt=F32):
            return ctx.enter_context(nc.sbuf_tensor(name, shape, dt))

        def sem(name):
            return ctx.enter_context(nc.semaphore(name))

        xs = sb("xs", [P, 2, TILES, C])
        stage = sb("stage", [P, 2, CHUNK, C])
        shiftb = sb("shiftb", [P, 4, C])
        q_junk = sb("q_junk", [P, 2, C], BF16)
        t_junk = sb("t_junk", [P, 2, C], BF16)
        partial = sb("partial", [P, C])
        diag = sb("diag", [P, J, P])
        u_row = sb("u_row", [P, 2, C])
        w_row = sb("w_row", [P, 2, C])
        wv = sb("wv", [P, J, D])
        wz = sb("wz", [P, H, C])
        wq2 = sb("wq2", [P, J, D])
        wv2t = sb("wv2t", [P, H, C])
        ident = sb("ident", [P, P])
        ones = sb("ones", [P, P])
        block16 = sb("block16", [P, P])
        sel = sb("sel", [P, 4])
        wq_col = sb("wq_col", [P, J])
        bv_col = sb("bv_col", [P, H])
        bz_col = sb("bz_col", [P, J])
        gamma = sb("gamma", [P, J])
        beta = sb("beta", [P, J])
        bv2_col = sb("bv2_col", [P, H])
        bq2_row = sb("bq2_row", [1, D])
        bq = sb("bq", [1, 1])
        stat = sb("stat", [P, 2, 2 * J])
        gstat = sb("gstat", [P, 2, 2 * J])
        m2 = sb("m2", [P, J])
        var = sb("var", [P, J])
        rs = sb("rs", [P, 2, J])
        wqs = sb("wqs", [P, J])
        mwq = sb("mwq", [P, J])
        qdot = sb("qdot", [P, TILES])
        logit = sb("logit", [P, TILES])
        lmax = sb("lmax", [P, 1])
        one_max = sb("one_max", [1, 1])
        neg_row = sb("neg_row", [1, P])
        neg_max = sb("neg_max", [P, 1])
        prob = sb("prob", [P, TILES])
        mass = sb("mass", [P, 1])
        inv_mass = sb("inv_mass", [P, 1])
        pool_n = sb("pool_n", [P, J])
        pool_y = sb("pool_y", [P, J])
        vcol = sb("vcol", [P, H])
        zcol = sb("zcol", [P, J])
        zmean = sb("zmean", [P, 1])
        zcent = sb("zcent", [P, J])
        zjunk = sb("zjunk", [P, J])
        zsq = sb("zsq", [P, 1])
        zvar = sb("zvar", [P, 1])
        zrstd = sb("zrstd", [P, 1])
        znorm = sb("znorm", [P, J])
        zgam = sb("zgam", [P, J])
        zbet = sb("zbet", [P, J])
        zexp = sb("zexp", [P, J])
        zden = sb("zden", [P, J])
        cw = sb("cw", [P, J])
        ucol = sb("ucol", [P, J])
        wcol = sb("wcol", [P, J])
        ycent = sb("ycent", [P, J])
        ymean = sb("ymean", [P, J])
        qrow = sb("qrow", [1, D])
        qmax = sb("qmax", [1, 1])
        arow = sb("arow", [1, D])
        asum = sb("asum", [1, 1])
        ainv = sb("ainv", [1, 1])
        acol = sb("acol", [P, H])
        kcol = sb("kcol", [P, J])
        terms = sb("terms", [P, J + H])
        shift = sb("shift", [P, 1])
        tdot = sb("tdot", [P, TILES])
        texp = sb("texp", [P, TILES])
        tden = sb("tden", [P, TILES])
        gate = sb("gate", [P, 2, TILES])
        halves = sb("halves", [P, J])

        def bank(name):
            return ctx.enter_context(nc.psum_tensor(name, [P, C], F32))

        gram_ps = bank("gram_ps")
        sum_ps = bank("sum_ps")
        weighted_ps = bank("weighted_ps")
        wq_ps = bank("wq_ps")
        v_ps = bank("v_ps")
        small = bank("small")
        gain_ps = [bank("gain0"), bank("gain1")]

        ev = {name: sem(name) for name in EVENTS}
        loaded = [[sem(f"loaded_{s}_{k}") for k in range(CHUNKS)] for s in range(2)]
        stored = [sem(f"stored_{s}") for s in range(2)]
        weights_in = sem("weights_in")
        made = sem("made")
        q_dotted = sem("q_dotted")
        t_dotted = sem("t_dotted")
        gate_exp = sem("gate_exp")
        gate_den = sem("gate_den")
        gate_done = sem("gate_done")
        gain_done = sem("gain_done")
        scaled = sem("scaled")
        added = sem("added")

        PAIRS = TILES // PAIR
        WEIGHTS = 12
        CONSTS = 9

        xv = x.rearrange("b h w c -> b (h w) c").rearrange("b (p t) c -> b p t c", p=P)
        ov = out.rearrange("b h w c -> b (h w) c").rearrange("b (p t) c -> b p t c", p=P)

        block = ctx.enter_context(nc.Block())

        def phases(engine, phase):
            phase(None, image(0, 0), image(0, 1))
            with engine.Fori(0, (IMAGES - 2) // 2) as i:
                phase(image(i, 0), image(i, 1), image(i, 2))
                phase(image(i, 1), image(i, 2), image(i, 3))
            last = IMAGES - 1
            phase(image(last // 2, 0), image(last // 2, 1), None)

        LAST = image((IMAGES - 1) // 2, 1)

        @block.sync
        def _(sp):
            def load(img, k):
                if not (isinstance(img.b, int) and img.b < 2):
                    sp.wait_ge(scaled, img.at(TILES, CHUNK * (k + 1) - 2 * TILES))
                sp.dma_start(xs[:, img.slot, k * CHUNK:(k + 1) * CHUNK, :],
                             xv[bass.ds(img.b, 1), :, k * CHUNK:(k + 1) * CHUNK, :].rearrange("o p t c -> (o p) t c")
                             ).then_inc(loaded[img.slot][k], 16)

            def store(img, k):
                sp.wait_ge(added, img.at(PAIRS, (k + 1) * CHUNK // PAIR))
                sp.dma_start(ov[bass.ds(img.b, 1), :, k * CHUNK:(k + 1) * CHUNK, :].rearrange("o p t c -> (o p) t c"),
                             stage[:, k % 2, :, :]).then_inc(stored[k % 2], 16)

            def phase(prev, cur, nxt):
                for k in range(CHUNKS):
                    if nxt:
                        load(nxt, k)
                    if prev:
                        store(prev, k)

            for k in range(CHUNKS):
                load(image(0, 0), k)
            phases(sp, phase)
            for k in range(CHUNKS):
                store(LAST, k)
            for s in range(2):
                sp.wait_ge(stored[s], 16 * IMAGES * CHUNKS // 2)

        @block.gpsimd
        def _(pool):
            nc.gpsimd.memset(ident[:], 0.0).then_inc(made, 1)
            nc.gpsimd.memset(ones[:], 1.0).then_inc(made, 1)
            nc.gpsimd.memset(block16[:], 1.0 / GROUP).then_inc(made, 1)
            nc.gpsimd.memset(sel[:, 0:1], 1.0 / (SW * TOKENS)).then_inc(made, 1)
            nc.gpsimd.memset(sel[:, 1:2], 1.0 / SW).then_inc(made, 1)
            nc.gpsimd.memset(neg_row[:], -1.0).then_inc(made, 1)
            nc.gpsimd.memset(halves[:], -0.5).then_inc(made, 1)
            pool.wait_ge(made, 7)
            nc.gpsimd.affine_select(out=ident[:], in_=ident[:], compare_op=ALU.not_equal, fill=1.0, base=0,
                                    pattern=[[-1, P]], channel_multiplier=1).then_inc(made, 1)
            blocks = block16[:].rearrange("p (g e) -> p g e", e=GROUP)
            nc.gpsimd.affine_select(out=blocks, in_=blocks, compare_op=ALU.is_ge, fill=0.0, base=0,
                                    pattern=[[-GROUP, P // GROUP], [0, GROUP]], channel_multiplier=1
                                    ).then_inc(made, 1)
            pool.wait_ge(made, CONSTS)
            nc.gpsimd.affine_select(out=blocks, in_=blocks, compare_op=ALU.is_ge, fill=0.0, base=GROUP - 1,
                                    pattern=[[GROUP, P // GROUP], [0, GROUP]], channel_multiplier=-1
                                    ).then_inc(made, 1)

            def add(img, lo, hi):
                for q in range(lo // PAIR, hi // PAIR):
                    t = q * PAIR
                    pool.wait_ge(scaled, img.at(TILES, t + PAIR))
                    pool.wait_ge(gain_done, img.at(TILES, t + PAIR))
                    k, r, s = t // CHUNK, t % CHUNK, t % 4
                    dst = stage[:, k % 2, r:r + PAIR, :]
                    nc.gpsimd.tensor_tensor(dst, dst, shiftb[:, s:s + PAIR, :], ALU.add).then_inc(added, 1)

            def group_power(img):
                pool.wait_ge(ev["stat_var"], img.b + 1)
                nc.gpsimd.tensor_tensor(rs[:, img.slot, :], var[:], halves[:], ALU.pow).then_inc(ev["rs"], 1)

            def layer_power(img):
                pool.wait_ge(ev["z_var"], img.b + 1)
                nc.gpsimd.tensor_tensor(zrstd[:], zvar[:], halves[:, 0:1], ALU.pow).then_inc(ev["z_rstd"], 1)

            def phase(prev, cur, nxt):
                if prev:
                    add(prev, 8, 24)
                layer_power(cur)
                if prev:
                    add(prev, 24, 32)
                add(cur, 0, 4)
                if nxt:
                    group_power(nxt)
                add(cur, 4, 8)

            group_power(image(0, 0))
            phases(pool, phase)
            add(LAST, 8, 32)

        @block.scalar
        def _(act):
            loads = [(wv[:], w["ch_wv_w"].rearrange("(j p) d -> p j d", p=P)),
                     (wz[:], w["ch_wz_w"].rearrange("(h p) c -> p h c", p=P)),
                     (wq2[:], w["sp_wq_w"].rearrange("(j p) d -> p j d", p=P)),
                     (wv2t[:], w["sp_wv_w_t"].rearrange("(h p) c -> p h c", p=P)),
                     (wq_col[:], w["ch_wq_w"]),
                     (bv_col[:], w["ch_wv_b"]),
                     (bz_col[:], w["ch_wz_b"]),
                     (gamma[:], w["ln_gamma"]),
                     (beta[:], w["ln_beta"]),
                     (bv2_col[:], w["sp_wv_b"]),
                     (bq2_row[:], w["sp_wq_b"].rearrange("(o d) -> o d", o=1)),
                     (bq[:], w["ch_wq_b"].rearrange("(o d) -> o d", o=1))]
            assert len(loads) == WEIGHTS
            for dst, src in loads:
                act.dma_start(dst, src).then_inc(weights_in, 16)

            def gains(img, lo, hi):
                for t in range(lo, hi):
                    s = gate[:, img.slot, t:t + 1]
                    if t % CHUNK == 0:
                        act.wait_ge(gate_done, img.at(CHUNKS, t // CHUNK + 1))
                    if t % PAIR == 0:
                        if comes(img.at(PAIRS, t // PAIR - 1)):
                            act.wait_ge(added, img.at(PAIRS, t // PAIR - 1))
                    nc.scalar.activation(shiftb[:, t % 4, :], w_row[:, img.slot, :], ACT.Copy, scale=s)
                    if comes(img.at(TILES, t - 1)):
                        act.wait_ge(scaled, img.at(TILES, t - 1))
                    nc.scalar.activation(gain_ps[t % 2][:], u_row[:, img.slot, :], ACT.Identity, scale=s,
                                         bias=1.0).then_inc(gain_done, 1)

            def gate_exps(img, k):
                act.wait_ge(t_dotted, img.at(TILES, (k + 1) * CHUNK))
                c = slice(k * CHUNK, (k + 1) * CHUNK)
                nc.scalar.activation(texp[:, c], tdot[:, c], ACT.Exp, scale=-1.0, bias=shift[:]
                                     ).then_inc(gate_exp, 1)

            def stats(img):
                act.wait_ge(ev["stat_ps"], img.b + 1)
                nc.scalar.activation(partial[:], sum_ps[:], ACT.Copy).then_inc(ev["sum_copied"], 1)

            def phase(prev, cur, nxt):
                if prev:
                    gains(prev, 8, 20)
                act.wait_ge(ev["max_neg"], cur.b + 1)
                nc.scalar.activation(prob[:], logit[:], ACT.Exp, bias=neg_max[:], accum_out=mass[:]
                                     ).then_inc(ev["probs"], 1)
                if prev:
                    gate_exps(prev, 3)
                    gains(prev, 20, 22)
                act.wait_ge(ev["weighted_ps"], cur.b + 1)
                nc.scalar.activation(partial[:], weighted_ps[:], ACT.Copy).then_inc(ev["weighted"], 1)
                if prev:
                    gains(prev, 22, 27)
                act.wait_ge(ev["z_beta"], cur.b + 1)
                nc.scalar.activation(zexp[:], zbet[:], ACT.Exp, scale=-1.0).then_inc(ev["z_exp"], 1)
                if prev:
                    gains(prev, 27, 29)
                act.wait_ge(ev["q_max"], cur.b + 1)
                nc.scalar.activation(arow[:], qrow[:], ACT.Exp, bias=qmax[:], accum_out=asum[:]
                                     ).then_inc(ev["q_exp"], 1)
                if prev:
                    gains(prev, 29, 32)
                for name, row in (("u", u_row), ("w", w_row)):
                    act.wait_ge(ev[f"{name}_ps"], cur.b + 1)
                    nc.scalar.activation(row[:, cur.slot, :], weighted_ps[:], ACT.Copy
                                         ).then_inc(ev[f"{name}_row"], 1)
                act.wait_ge(ev["shift"], cur.b + 1)
                gate_exps(cur, 0)
                gate_exps(cur, 1)
                gains(cur, 0, 2)
                gate_exps(cur, 2)
                gains(cur, 2, 4)
                if nxt:
                    stats(nxt)
                gains(cur, 4, 8)

            stats(image(0, 0))
            phases(act, phase)
            gains(LAST, 8, 20)
            gate_exps(LAST, 3)
            gains(LAST, 20, 32)

        @block.tensor
        def _(pe):
            pe.wait_ge(made, CONSTS + 1)
            pe.wait_ge(weights_in, 16 * WEIGHTS)

            def gram(img, lo, hi):
                for t in range(lo, hi):
                    if t % CHUNK == 0:
                        pe.wait_ge(loaded[img.slot][t // CHUNK], img.use * 16 + 16)
                    if t == 0:
                        if comes(img.at(1, 0)):
                            pe.wait_ge(ev["square_col"], img.at(1, 0))
                        if comes(img.at(1, 0)):
                            pe.wait_ge(ev["sum_copied"], img.at(1, 0))
                    tile = xs[:, img.slot, t, :]
                    s = (t % STRIPS) * SW
                    nc.tensor.matmul(sum_ps[s:s + SW, :], ones[:, 0:SW], tile, start=t < STRIPS,
                                     stop=t >= TILES - STRIPS)
                    for j in range(J):
                        cols = slice(j * P, (j + 1) * P)
                        last = nc.tensor.matmul(gram_ps[:, cols], tile[:, cols], tile[:, cols],
                                                start=t == 0 and j == 0, stop=t == TILES - 1 and j == J - 1,
                                                skip_group_check=True)
                    if t == TILES - 1:
                        last.then_inc(ev["stat_ps"], 1)

            def row(dst, column_diag):
                return nc.tensor.matmul(dst[:], ones[:], column_diag[:].rearrange("p j c -> p (j c)"),
                                        start=True, stop=True)

            def stats(img):
                pe.wait_ge(ev["sum_copied"], img.b + 1)
                for j in range(J):
                    last = nc.tensor.matmul(small[:, j:j + 1], partial[:, j * P:(j + 1) * P], sel[:, 0:1],
                                            start=True, stop=True)
                last.then_inc(ev["stat_group_ps"], 1)
                pe.wait_ge(ev["stat_mean"], img.b + 1)
                pe.wait_ge(ev["square_col"], img.b + 1)
                nc.tensor.matmul(small[:, 8:8 + 2 * J], block16[:], stat[:, img.slot, :], start=True,
                                        stop=True).then_inc(ev["stat_group"], 1)
                pe.wait_ge(ev["mwq_col"], img.b + 1)
                for j in range(J):
                    nc.tensor.matmul(small[:, 16:17], ones[:], mwq[:, j:j + 1], start=j == 0, stop=False)
                nc.tensor.matmul(small[:, 16:17], ones[0:1, :], bq[:], start=False, stop=True)
                pe.wait_ge(ev["wq_diag"], img.b + 1)
                row(wq_ps, diag).then_inc(ev["wq_row"], 1)

            def softmax(cur):
                pe.wait_ge(ev["logits_max"], cur.b + 1)
                nc.tensor.transpose(small[0:1, P:2 * P], lmax[:], ident[:]).then_inc(ev["max_t"], 1)
                pe.wait_ge(ev["max_one"], cur.b + 1)
                nc.tensor.matmul(small[:, 17:18], neg_row[:], one_max[:], start=True, stop=True).then_inc(ev["max_ps"], 1)
                pe.wait_ge(ev["probs"], cur.b + 1)
                nc.tensor.matmul(small[:, 18:19], ones[:], mass[:], start=True, stop=True).then_inc(ev["mass_ps"], 1)
                for t in range(TILES):
                    s = (t % STRIPS) * SW
                    last = nc.tensor.matmul(weighted_ps[s:s + SW, :], prob[:, t:t + 1].to_broadcast([P, SW]),
                                            xs[:, cur.slot, t, :], start=t < STRIPS, stop=t >= TILES - STRIPS)
                last.then_inc(ev["weighted_ps"], 1)

            def columns(dst, weight, rhs, blocks, depth):
                for o in range(blocks):
                    for i in range(depth):
                        last = nc.tensor.matmul(dst[:, o:o + 1], weight[:, i, o * P:(o + 1) * P], rhs[:, i:i + 1],
                                                start=i == 0, stop=i == depth - 1)
                return last

            def channel(cur, fill):
                pe.wait_ge(ev["weighted"], cur.b + 1)
                pe.wait_ge(ev["mass_inv"], cur.b + 1)
                for j in range(J):
                    last = nc.tensor.matmul(small[:, 20 + j:21 + j], partial[:, j * P:(j + 1) * P],
                                            sel[:, 1:2], start=True, stop=True)
                last.then_inc(ev["pooled_ps"], 1)
                fill(8, 9)
                pe.wait_ge(ev["pooled"], cur.b + 1)
                columns(small[:, 24:24 + H], wv, pool_y, H, J).then_inc(ev["v_ps"], 1)
                fill(9, 10)
                pe.wait_ge(ev["v"], cur.b + 1)
                columns(small[:, 28:28 + J], wz, vcol, J, H).then_inc(ev["z_ps"], 1)
                fill(10, 11)
                pe.wait_ge(ev["z"], cur.b + 1)
                nc.tensor.matmul(small[:, 32:32 + J], ones[:], zcol[:], start=True, stop=True).then_inc(ev["z_mean_ps"], 1)
                fill(11, 12)
                pe.wait_ge(ev["z_sq"], cur.b + 1)
                nc.tensor.matmul(small[:, 36:37], ones[:], zsq[:], start=True, stop=True).then_inc(ev["z_var_ps"], 1)
                fill(12, 14)

            def spatial(cur, fill):
                pe.wait_ge(ev["y_mean"], cur.b + 1)
                for j in range(J):
                    last = nc.tensor.matmul(small[0:1, D:2 * D], ymean[:, j:j + 1], wq2[:, j, :], start=j == 0,
                                            stop=j == J - 1)
                last.then_inc(ev["q_ps"], 1)
                fill(14, 15)
                pe.wait_ge(ev["q_inv"], cur.b + 1)
                for h in range(H):
                    last = nc.tensor.matmul(small[:, 40 + h:41 + h], arow[:, h * P:(h + 1) * P], ainv[:],
                                            start=True, stop=True)
                last.then_inc(ev["a_ps"], 1)
                fill(15, 16)
                pe.wait_ge(ev["a"], cur.b + 1)
                columns(small[:, 44:44 + J], wv2t, acol, J, H).then_inc(ev["k_ps"], 1)
                pe.wait_ge(ev["v_diag"], cur.b + 1)
                row(v_ps, diag).then_inc(ev["v_row"], 1)
                pe.wait_ge(ev["shift_b"], cur.b + 1)
                for j in range(J + H):
                    last = nc.tensor.matmul(small[:, 48:49], ones[:], terms[:, j:j + 1], start=j == 0,
                                            stop=j == J + H - 1)
                last.then_inc(ev["shift_ps"], 1)
                pe.wait_ge(ev["u_diag"], cur.b + 1)
                row(weighted_ps, diag).then_inc(ev["u_ps"], 1)
                pe.wait_ge(ev["w_diag"], cur.b + 1)
                pe.wait_ge(ev["u_row"], cur.b + 1)
                row(weighted_ps, diag).then_inc(ev["w_ps"], 1)

            def phase(prev, cur, nxt):
                def fill(lo, hi):
                    if nxt:
                        gram(nxt, lo, hi)

                fill(0, 8)
                softmax(cur)
                channel(cur, fill)
                spatial(cur, fill)
                fill(16, TILES)
                if nxt:
                    stats(nxt)

            gram(image(0, 0), 0, TILES)
            stats(image(0, 0))
            phases(pe, phase)

        @block.vector
        def _(dve):
            dve.wait_ge(made, CONSTS + 1)
            dve.wait_ge(weights_in, 16 * WEIGHTS)
            v = nc.vector

            def dots(img, lo, hi, row_ps, dst, junk, dotted):
                for t in range(lo, hi):
                    if comes(img.at(TILES, t - 1)):
                        dve.wait_ge(dotted, img.at(TILES, t - 1))
                    v.tensor_tensor_reduce(out=junk[:, t % 2, :], in0=xs[:, img.slot, t, :], in1=row_ps[:],
                                           scale=1.0, scalar=0.0, op0=ALU.mult, op1=ALU.add,
                                           accum_out=dst[:, t:t + 1]).then_inc(dotted, 1)

            def q_dots(img, lo, hi):
                dots(img, lo, hi, wq_ps, qdot, q_junk, q_dotted)

            def gate_dots(img, lo, hi):
                dots(img, lo, hi, v_ps, tdot, t_junk, t_dotted)

            def gates(img, k):
                c = slice(k * CHUNK, (k + 1) * CHUNK)
                dve.wait_ge(gate_exp, img.at(CHUNKS, k + 1))
                v.tensor_scalar(tden[:, c], texp[:, c], 1.0, None, ALU.add).then_inc(gate_den, 1)
                dve.wait_ge(gate_den, img.at(CHUNKS, k + 1))
                v.reciprocal(gate[:, img.slot, c], tden[:, c]).then_inc(gate_done, 1)

            def scale(img, lo, hi):
                for t in range(lo, hi):
                    k, r = t // CHUNK, t % CHUNK
                    if r == 0:
                        if comes(img.at(16 * CHUNKS // 2, 16 * (k // 2))):
                            dve.wait_ge(stored[k % 2], img.at(16 * CHUNKS // 2, 16 * (k // 2)))
                    dve.wait_ge(gain_done, img.at(TILES, t + 1))
                    v.tensor_tensor(stage[:, k % 2, r, :], xs[:, img.slot, t, :], gain_ps[t % 2][:],
                                    ALU.mult).then_inc(scaled, 1)

            def diagonal(column, img, name):
                ins = v.tensor_tensor(diag[:], ident[:].unsqueeze(1).to_broadcast([P, J, P]),
                                      column.unsqueeze(2).to_broadcast([P, J, P]), ALU.mult)
                ins.then_inc(ev[name], 1)

            def stats(img, fill):
                dve.wait_ge(ev["stat_ps"], img.b + 1)
                for j in range(J):
                    last = v.tensor_tensor_reduce(out=diag[:, j, :],
                                                  in0=gram_ps[:, j * P:(j + 1) * P], in1=ident[:],
                                                  scale=1.0 / TOKENS, scalar=0.0, op0=ALU.mult, op1=ALU.add,
                                                  accum_out=stat[:, img.slot, J + j:J + j + 1])
                last.then_inc(ev["square_col"], 1)
                dve.wait_ge(ev["square_col"], img.b + 1)
                dve.wait_ge(ev["stat_group_ps"], img.b + 1)
                v.tensor_copy(stat[:, img.slot, 0:J], small[:, 0:J]).then_inc(ev["stat_mean"], 1)
                fill(4, 5)
                dve.wait_ge(ev["stat_group"], img.b + 1)
                g = gstat[:, img.slot, :]
                v.tensor_copy(g, small[:, 8:8 + 2 * J]).then_inc(ev["stat_group_sb"], 1)
                dve.wait_ge(ev["stat_group_sb"], img.b + 1)
                v.tensor_tensor(m2[:], g[:, 0:J], g[:, 0:J], ALU.mult).then_inc(ev["stat_m2"], 1)
                dve.wait_ge(ev["stat_m2"], img.b + 1)
                v.scalar_tensor_tensor(out=var[:], in0=g[:, J:2 * J], scalar=GN_EPS, in1=m2[:], op0=ALU.add,
                                            op1=ALU.subtract).then_inc(ev["stat_var"], 1)
                dve.wait_ge(ev["stat_var"], img.b + 1)
                fill(5, 7)
                dve.wait_ge(ev["rs"], img.b + 1)
                v.tensor_tensor(wqs[:], wq_col[:], rs[:, img.slot, :], ALU.mult).then_inc(ev["wq_col"], 1)
                dve.wait_ge(ev["wq_col"], img.b + 1)
                diagonal(wqs[:], img, "wq_diag")
                v.scalar_tensor_tensor(out=mwq[:], in0=g[:, 0:J], scalar=-1.0, in1=wqs[:], op0=ALU.mult,
                                       op1=ALU.mult).then_inc(ev["mwq_col"], 1)
                fill(7, 8)

            def phase(prev, cur, nxt):
                def fill_prev(lo, hi):
                    if prev:
                        scale(prev, lo, hi)

                m = gstat[:, cur.slot, 0:J]
                r = rs[:, cur.slot, :]
                dve.wait_ge(ev["wq_row"], cur.b + 1)
                for n in range(12):
                    q_dots(cur, n * TILES // 12, (n + 1) * TILES // 12)
                    fill_prev(8 + n, 9 + n)
                dve.wait_ge(q_dotted, cur.at(TILES, TILES))
                v.tensor_scalar(logit[:], qdot[:], small[:, 16:17], None, ALU.add, ALU.max,
                                     accum_out=lmax[:]).then_inc(ev["logits_max"], 1)
                dve.wait_ge(ev["logits_max"], cur.b + 1)
                if prev:
                    gate_dots(prev, 24, 26)
                dve.wait_ge(ev["max_t"], cur.b + 1)
                v.tensor_reduce(one_max[:], small[0:1, P:2 * P], AX.X, ALU.max).then_inc(ev["max_one"], 1)
                if prev:
                    gate_dots(prev, 26, 27)
                dve.wait_ge(ev["max_ps"], cur.b + 1)
                v.tensor_copy(neg_max[:], small[:, 17:18]).then_inc(ev["max_neg"], 1)
                if prev:
                    gate_dots(prev, 27, 32)
                dve.wait_ge(ev["mass_ps"], cur.b + 1)
                v.reciprocal(inv_mass[:], small[:, 18:19]).then_inc(ev["mass_inv"], 1)
                if prev:
                    gates(prev, 3)
                fill_prev(20, 22)
                dve.wait_ge(ev["pooled_ps"], cur.b + 1)
                dve.wait_ge(ev["mass_inv"], cur.b + 1)
                v.scalar_tensor_tensor(out=pool_n[:], in0=small[:, 20:20 + J], scalar=inv_mass[:], in1=m,
                                            op0=ALU.mult, op1=ALU.subtract).then_inc(ev["pooled_n"], 1)
                dve.wait_ge(ev["pooled_n"], cur.b + 1)
                v.tensor_tensor(pool_y[:], pool_n[:], r, ALU.mult).then_inc(ev["pooled"], 1)
                dve.wait_ge(ev["pooled"], cur.b + 1)
                fill_prev(22, 23)
                dve.wait_ge(ev["v_ps"], cur.b + 1)
                v.tensor_tensor(vcol[:], small[:, 24:24 + H], bv_col[:], ALU.add).then_inc(ev["v"], 1)
                fill_prev(23, 24)
                dve.wait_ge(ev["z_ps"], cur.b + 1)
                v.tensor_tensor(zcol[:], small[:, 28:28 + J], bz_col[:], ALU.add).then_inc(ev["z"], 1)
                dve.wait_ge(ev["z"], cur.b + 1)
                fill_prev(24, 25)
                dve.wait_ge(ev["z_mean_ps"], cur.b + 1)
                v.tensor_reduce(zmean[:], small[:, 32:32 + J], AX.X, ALU.add).then_inc(ev["z_mean"], 1)
                dve.wait_ge(ev["z_mean"], cur.b + 1)
                v.scalar_tensor_tensor(out=zcent[:], in0=zmean[:].to_broadcast([P, J]), scalar=-1.0 / C,
                                            in1=zcol[:], op0=ALU.mult, op1=ALU.add).then_inc(ev["z_cent"], 1)
                dve.wait_ge(ev["z_cent"], cur.b + 1)
                v.tensor_tensor_reduce(out=zjunk[:], in0=zcent[:], in1=zcent[:], scale=1.0 / C, scalar=0.0,
                                       op0=ALU.mult, op1=ALU.add, accum_out=zsq[:]).then_inc(ev["z_sq"], 1)
                fill_prev(25, 26)
                dve.wait_ge(ev["z_var_ps"], cur.b + 1)
                v.tensor_scalar(zvar[:], small[:, 36:37], LN_EPS, None, ALU.add).then_inc(ev["z_var"], 1)
                dve.wait_ge(ev["z_var"], cur.b + 1)
                fill_prev(26, 27)
                dve.wait_ge(ev["z_rstd"], cur.b + 1)
                v.tensor_scalar(znorm[:], zcent[:], zrstd[:], None, ALU.mult).then_inc(ev["z_norm"], 1)
                dve.wait_ge(ev["z_norm"], cur.b + 1)
                v.tensor_tensor(zgam[:], znorm[:], gamma[:], ALU.mult).then_inc(ev["z_gamma"], 1)
                dve.wait_ge(ev["z_gamma"], cur.b + 1)
                v.tensor_tensor(zbet[:], zgam[:], beta[:], ALU.add).then_inc(ev["z_beta"], 1)
                dve.wait_ge(ev["z_beta"], cur.b + 1)
                v.tensor_tensor(ycent[:], stat[:, cur.slot, 0:J], m, ALU.subtract).then_inc(ev["y_cent"], 1)
                dve.wait_ge(ev["y_cent"], cur.b + 1)
                dve.wait_ge(ev["z_exp"], cur.b + 1)
                v.tensor_scalar(zden[:], zexp[:], 1.0, None, ALU.add).then_inc(ev["z_den"], 1)
                dve.wait_ge(ev["z_den"], cur.b + 1)
                v.reciprocal(cw[:], zden[:]).then_inc(ev["cw"], 1)
                dve.wait_ge(ev["cw"], cur.b + 1)
                v.tensor_tensor(ucol[:], cw[:], r, ALU.mult).then_inc(ev["u"], 1)
                dve.wait_ge(ev["u"], cur.b + 1)
                v.tensor_tensor(ymean[:], ycent[:], ucol[:], ALU.mult).then_inc(ev["y_mean"], 1)
                v.scalar_tensor_tensor(out=wcol[:], in0=ucol[:], scalar=-1.0, in1=m, op0=ALU.mult,
                                            op1=ALU.mult).then_inc(ev["w"], 1)
                dve.wait_ge(ev["w"], cur.b + 1)
                fill_prev(27, 28)
                dve.wait_ge(ev["q_ps"], cur.b + 1)
                v.tensor_tensor(qrow[:], small[0:1, D:2 * D], bq2_row[:], ALU.add).then_inc(ev["q_row"], 1)
                dve.wait_ge(ev["q_row"], cur.b + 1)
                v.tensor_reduce(qmax[:], qrow[:], AX.X, ALU.max, negate=True).then_inc(ev["q_max"], 1)
                dve.wait_ge(ev["q_max"], cur.b + 1)
                fill_prev(28, 29)
                dve.wait_ge(ev["q_exp"], cur.b + 1)
                v.reciprocal(ainv[:], asum[:]).then_inc(ev["q_inv"], 1)
                fill_prev(29, 30)
                dve.wait_ge(ev["a_ps"], cur.b + 1)
                v.tensor_copy(acol[:], small[:, 40:40 + H]).then_inc(ev["a"], 1)
                dve.wait_ge(ev["a"], cur.b + 1)
                fill_prev(30, 31)
                dve.wait_ge(ev["k_ps"], cur.b + 1)
                v.tensor_tensor(kcol[:], small[:, 44:44 + J], ucol[:], ALU.mult).then_inc(ev["v_col"], 1)
                dve.wait_ge(ev["v_col"], cur.b + 1)
                diagonal(kcol[:], cur, "v_diag")
                v.tensor_tensor(terms[:, 0:J], kcol[:], m, ALU.mult).then_inc(ev["shift_a"], 1)
                dve.wait_ge(ev["shift_a"], cur.b + 1)
                v.scalar_tensor_tensor(out=terms[:, J:J + H], in0=acol[:], scalar=-1.0, in1=bv2_col[:],
                                       op0=ALU.mult, op1=ALU.mult).then_inc(ev["shift_b"], 1)
                fill_prev(31, 32)
                dve.wait_ge(ev["v_row"], cur.b + 1)
                diagonal(ucol[:], cur, "u_diag")
                dve.wait_ge(ev["shift_ps"], cur.b + 1)
                v.tensor_copy(shift[:], small[:, 48:49]).then_inc(ev["shift"], 1)
                gate_dots(cur, 0, 8)
                dve.wait_ge(ev["u_ps"], cur.b + 1)
                diagonal(wcol[:], cur, "w_diag")
                gates(cur, 0)
                gate_dots(cur, 8, 16)
                gates(cur, 1)
                scale(cur, 0, 2)
                gate_dots(cur, 16, 24)
                gates(cur, 2)
                scale(cur, 2, 4)
                if nxt:
                    dve.wait_ge(ev["w_ps"], cur.b + 1)
                    stats(nxt, lambda lo, hi: scale(cur, lo, hi))
                else:
                    scale(cur, 4, 8)

            stats(image(0, 0), lambda lo, hi: None)
            phases(dve, phase)
            scale(LAST, 8, 20)
            gate_dots(LAST, 24, 32)
            gates(LAST, 3)
            scale(LAST, 20, 32)


def kernel(**inputs):
    import numpy as np
    import concourse.bacc as bacc
    from concourse.bass_utils import run_bass_kernel_spmd as run

    nc = bacc.Bacc("TRN2", target_bir_lowering=False, num_devices=1)
    arrays = {"x": np.ascontiguousarray(inputs["x"])}
    for name in ("ch_wv_w", "ch_wv_b", "ch_wq_w", "ch_wq_b", "ch_wz_w", "ch_wz_b", "ln_gamma", "ln_beta",
                 "sp_wv_b", "sp_wq_w", "sp_wq_b"):
        arrays[name] = np.ascontiguousarray(inputs[f"L0_conv_{name}"])
    for name in ("ch_wq_w", "ch_wv_b", "ch_wz_b", "ln_gamma", "ln_beta", "sp_wv_b"):
        arrays[name] = np.ascontiguousarray(np.transpose(np.reshape(arrays[name], (-1, P))))
    arrays["sp_wv_w_t"] = np.ascontiguousarray(np.transpose(inputs["L0_conv_sp_wv_w"]))
    w = {name: nc.dram_tensor(name, a.shape, mybir.dt.from_np(a.dtype), kind="ExternalInput").ap()
         for name, a in arrays.items()}
    out = nc.dram_tensor("out", arrays["x"].shape, F32, kind="ExternalOutput").ap()
    build(nc, w["x"], w, out)
    return run(nc, [arrays], core_ids=[0]).results[0]["out"]
```

```python
from contextlib import ExitStack

import concourse.bass as bass
from concourse import mybir

F32 = mybir.dt.float32
BF16 = mybir.dt.bfloat16
ALU = mybir.AluOpType
ACT = mybir.ActivationFunctionType
AX = mybir.AxisListType

P = 128
IMAGES, TOKENS, C = 16, 64 * 64, 512
TILES = TOKENS // P
J = C // P
D = C // 2
H = D // P
GROUP = 16
CHUNK = 8
QUAD = 4
QUADS = TILES // QUAD
CHUNKS = TILES // CHUNK
STRIPS = 4
SW = P // STRIPS
GN_EPS, LN_EPS = 1e-5, 1e-3

EVENTS = (
    "sum_copied", "square_col", "stat_ps", "stat_mean", "stat_group_ps", "stat_group", "stat_group_sb", "stat_m2",
    "stat_var", "rs", "wq_col", "mwq_col", "wq_diag", "wq_row",
    "logits_max", "max_t", "max_one", "max_ps", "max_neg", "probs",
    "weighted_ps", "mass_ps", "weighted", "mass_inv", "pooled_ps", "pooled_n", "pooled",
    "z_ps", "z", "z_sq", "z_var_ps", "z_var", "z_rstd", "z_gamma", "z_beta", "z_exp", "z_den", "cw", "u", "w",
    "y_cent", "y_mean", "q_ps", "q_row", "q_max", "q_exp", "q_inv", "a_ps", "a", "k_ps", "v_col",
    "shift_a", "shift_b", "shift_ps", "shift", "v_diag", "v_row", "u_diag", "u_ps", "u_row", "w_diag", "w_ps",
    "w_row",
)


class Image:

    def __init__(self, b, slot, use):
        self.b, self.slot, self.use = b, slot, use

    def at(self, count, n):
        return self.b * count + n


def comes(value):
    return not isinstance(value, int) or value > 0


def image(i, off):
    return Image(i * 2 + off, off % 2, i + off // 2)


def build(nc, x, w, out):
    ctx = ExitStack()
    with ctx:
        def sb(name, shape, dt=F32):
            return ctx.enter_context(nc.sbuf_tensor(name, shape, dt))

        def sem(name):
            return ctx.enter_context(nc.semaphore(name))

        xs = sb("xs", [P, 2, TILES, C])
        stage = sb("stage", [P, 2, CHUNK, C])
        shiftb = sb("shiftb", [P, 4, C])
        q_junk = sb("q_junk", [P, 2, C], BF16)
        t_junk = sb("t_junk", [P, 2, C], BF16)
        partial = sb("partial", [P, C])
        diag = sb("diag", [P, J, P])
        u_row = sb("u_row", [P, 2, C])
        w_row = sb("w_row", [P, 2, C])
        wvz = sb("wvz", [P, J, C])
        wvz_sum = sb("wvz_sum", [P, J])
        wvz_mean = sb("wvz_mean", [P, J])
        wq2 = sb("wq2", [P, J, D])
        wv2t = sb("wv2t", [P, H, C])
        ident = sb("ident", [P, P])
        ones = sb("ones", [P, P])
        block16 = sb("block16", [P, P])
        sel = sb("sel", [P, 4])
        wq_col = sb("wq_col", [P, J])
        bv_col = sb("bv_col", [P, H])
        bz_col = sb("bz_col", [P, J])
        gamma = sb("gamma", [P, J])
        beta = sb("beta", [P, J])
        bv2_col = sb("bv2_col", [P, H])
        bq2_row = sb("bq2_row", [1, D])
        bq = sb("bq", [P, 1])
        bq_part = sb("bq_part", [P, 1])
        stat = sb("stat", [P, 2, 2 * J])
        gstat = sb("gstat", [P, 2, 2 * J])
        m2 = sb("m2", [P, J])
        var = sb("var", [P, J])
        rs = sb("rs", [P, 2, J])
        wqs = sb("wqs", [P, J])
        mwq = sb("mwq", [P, J])
        mwq_sum = sb("mwq_sum", [P, 1])
        qdot = sb("qdot", [P, TILES])
        logit = sb("logit", [P, TILES])
        lmax = sb("lmax", [P, 1])
        one_max = sb("one_max", [1, 1])
        neg_row = sb("neg_row", [1, P])
        neg_max = sb("neg_max", [P, 1])
        prob = sb("prob", [P, TILES])
        mass = sb("mass", [P, 1])
        inv_mass = sb("inv_mass", [P, 1])
        pool_n = sb("pool_n", [P, J])
        pool_y = sb("pool_y", [P, J])
        bvz = sb("bvz", [P, J])
        bvz_sum = sb("bvz_sum", [P, 1])
        bvz_mean = sb("bvz_mean", [P, 1])
        zcent = sb("zcent", [P, J])
        zjunk = sb("zjunk", [P, J])
        zsq = sb("zsq", [P, 1])
        zvar = sb("zvar", [P, 1])
        zrstd = sb("zrstd", [P, 1])
        zgam = sb("zgam", [P, J])
        zbet = sb("zbet", [P, J])
        zexp = sb("zexp", [P, J])
        zden = sb("zden", [P, J])
        cw = sb("cw", [P, J])
        ucol = sb("ucol", [P, J])
        wcol = sb("wcol", [P, J])
        ycent = sb("ycent", [P, J])
        ymean = sb("ymean", [P, J])
        qrow = sb("qrow", [1, D])
        qmax = sb("qmax", [1, 1])
        arow = sb("arow", [1, D])
        asum = sb("asum", [1, 1])
        ainv = sb("ainv", [1, 1])
        acol = sb("acol", [P, H])
        kcol = sb("kcol", [P, J])
        terms = sb("terms", [P, J])
        vm = sb("vm", [P, 1])
        vm_ab = sb("vm_ab", [P, 1])
        shift = sb("shift", [P, 1])
        tdot = sb("tdot", [P, TILES])
        texp = sb("texp", [P, TILES])
        tden = sb("tden", [P, TILES])
        gate = sb("gate", [P, 2, TILES])
        halves = sb("halves", [P, J])

        def bank(name):
            return ctx.enter_context(nc.psum_tensor(name, [P, C], F32))

        gram_ps = bank("gram_ps")
        sum_ps = bank("sum_ps")
        weighted_ps = bank("weighted_ps")
        wq_ps = bank("wq_ps")
        v_ps = bank("v_ps")
        small = bank("small")
        gain_ps = [bank("gain0"), bank("gain1")]

        ev = {name: sem(name) for name in EVENTS}
        loaded = [[sem(f"loaded_{s}_{k}") for k in range(QUADS)] for s in range(2)]
        stored = [sem(f"stored_{s}") for s in range(2)]
        vectors_in = sem("vectors_in")
        weights_in = sem("weights_in")
        spatial_in = sem("spatial_in")
        product_ps = sem("product_ps")
        product_sum = sem("product_sum")
        product_mean = sem("product_mean")
        product = sem("product")
        bias_ps = sem("bias_ps")
        bias = sem("bias")
        bq_parted = sem("bq_parted")
        made = sem("made")
        q_dotted = sem("q_dotted")
        t_dotted = sem("t_dotted")
        gate_exp = sem("gate_exp")
        gate_den = sem("gate_den")
        gate_done = sem("gate_done")
        gain_done = sem("gain_done")
        scaled = sem("scaled")
        added = sem("added")

        CONSTS = 9

        xv = x.rearrange("b h w c -> b (h w) c").rearrange("b (p t) c -> b p t c", p=P)
        ov = out.rearrange("b h w c -> b (h w) c").rearrange("b (p t) c -> b p t c", p=P)

        wv_t = stage[:, 0, 0:H, :]
        wz = stage[:, 0, H:2 * H, :]

        block = ctx.enter_context(nc.Block())

        def phases(engine, phase):
            phase(None, image(0, 0), image(0, 1))
            with engine.Fori(0, (IMAGES - 2) // 2) as i:
                phase(image(i, 0), image(i, 1), image(i, 2))
                phase(image(i, 1), image(i, 2), image(i, 3))
            last = IMAGES - 1
            phase(image(last // 2, 0), image(last // 2, 1), None)

        LAST = image((IMAGES - 1) // 2, 1)

        @block.sync
        def _(sp):
            def load(img, q):
                tiles = slice(q * QUAD, (q + 1) * QUAD)
                if not (isinstance(img.b, int) and img.b < 2):
                    sp.wait_ge(scaled, img.at(TILES, QUAD * (q + 1) - 2 * TILES))
                sp.dma_start(xs[:, img.slot, tiles, :],
                             xv[bass.ds(img.b, 1), :, tiles, :].rearrange("o p t c -> (o p) t c")
                             ).then_inc(loaded[img.slot][q], 16)

            def store(img, k):
                sp.wait_ge(added, img.at(TILES, (k + 1) * CHUNK))
                sp.dma_start(ov[bass.ds(img.b, 1), :, k * CHUNK:(k + 1) * CHUNK, :].rearrange("o p t c -> (o p) t c"),
                             stage[:, k % 2, :, :]).then_inc(stored[k % 2], 16)

            def phase(prev, cur, nxt):
                for k in range(CHUNKS):
                    if nxt:
                        load(nxt, 2 * k)
                        load(nxt, 2 * k + 1)
                    if prev:
                        store(prev, k)

            for dst, src in ((wq_col, w["ch_wq_w"]), (bv_col, w["ch_wv_b"]), (bz_col, w["ch_wz_b"]),
                             (gamma, w["ln_gamma"]), (beta, w["ln_beta"]), (bv2_col, w["sp_wv_b"]),
                             (bq2_row, w["sp_wq_b"].rearrange("(o d) -> o d", o=1)),
                             (bq, w["ch_wq_b"].rearrange("(o d) -> o d", o=1).to_broadcast([P, 1]))):
                sp.dma_start(dst[:], src).then_inc(vectors_in, 16)
            for q in range(QUADS):
                load(image(0, 0), q)
            sp.dma_start(wv_t, w["ch_wv_w_t"].rearrange("(h p) c -> p h c", p=P)).then_inc(weights_in, 16)
            sp.dma_start(wz, w["ch_wz_w"].rearrange("(h p) c -> p h c", p=P)).then_inc(weights_in, 16)
            sp.dma_start(wq2[:], w["sp_wq_w"].rearrange("(j p) d -> p j d", p=P)).then_inc(spatial_in, 16)
            sp.dma_start(wv2t[:], w["sp_wv_w_t"].rearrange("(h p) c -> p h c", p=P)).then_inc(spatial_in, 16)
            phases(sp, phase)
            for k in range(CHUNKS):
                store(LAST, k)
            for s in range(2):
                sp.wait_ge(stored[s], 16 * IMAGES * CHUNKS // 2)

        @block.gpsimd
        def _(pool):
            nc.gpsimd.memset(ident[:], 0.0).then_inc(made, 1)
            nc.gpsimd.memset(ones[:], 1.0).then_inc(made, 1)
            nc.gpsimd.memset(block16[:], 1.0 / GROUP).then_inc(made, 1)
            nc.gpsimd.memset(sel[:, 0:1], 1.0 / (SW * TOKENS)).then_inc(made, 1)
            nc.gpsimd.memset(sel[:, 1:2], 1.0 / SW).then_inc(made, 1)
            nc.gpsimd.memset(neg_row[:], -1.0).then_inc(made, 1)
            nc.gpsimd.memset(halves[:], -0.5).then_inc(made, 1)
            pool.wait_ge(made, 7)
            nc.gpsimd.affine_select(out=ident[:], in_=ident[:], compare_op=ALU.not_equal, fill=1.0, base=0,
                                    pattern=[[-1, P]], channel_multiplier=1).then_inc(made, 1)
            blocks = block16[:].rearrange("p (g e) -> p g e", e=GROUP)
            nc.gpsimd.affine_select(out=blocks, in_=blocks, compare_op=ALU.is_ge, fill=0.0, base=0,
                                    pattern=[[-GROUP, P // GROUP], [0, GROUP]], channel_multiplier=1
                                    ).then_inc(made, 1)
            pool.wait_ge(made, CONSTS)
            nc.gpsimd.affine_select(out=blocks, in_=blocks, compare_op=ALU.is_ge, fill=0.0, base=GROUP - 1,
                                    pattern=[[GROUP, P // GROUP], [0, GROUP]], channel_multiplier=-1
                                    ).then_inc(made, 1)

            def add(img, lo, hi):
                for t in range(lo, hi):
                    pool.wait_ge(scaled, img.at(TILES, t + 1))
                    pool.wait_ge(gain_done, img.at(TILES, t + 1))
                    dst = stage[:, t // CHUNK % 2, t % CHUNK, :]
                    nc.gpsimd.tensor_tensor(dst, dst, shiftb[:, t % 4, :], ALU.add).then_inc(added, 1)

            def group_power(img):
                pool.wait_ge(ev["stat_var"], img.b + 1)
                nc.gpsimd.tensor_tensor(rs[:, img.slot, :], var[:], halves[:], ALU.pow).then_inc(ev["rs"], 1)

            def layer_power(img):
                pool.wait_ge(ev["z_var"], img.b + 1)
                nc.gpsimd.tensor_tensor(zrstd[:], zvar[:], halves[:, 0:1], ALU.pow).then_inc(ev["z_rstd"], 1)

            def phase(prev, cur, nxt):
                if prev:
                    add(prev, 8, 21)
                layer_power(cur)
                if prev:
                    add(prev, 21, 32)
                add(cur, 0, 6)
                if nxt:
                    group_power(nxt)
                add(cur, 6, 8)

            group_power(image(0, 0))
            phases(pool, phase)
            add(LAST, 8, 32)

        @block.scalar
        def _(act):
            def gains(img, lo, hi):
                for t in range(lo, hi):
                    s = gate[:, img.slot, t:t + 1]
                    if t % CHUNK == 0:
                        act.wait_ge(gate_done, img.at(CHUNKS, t // CHUNK + 1))
                    if comes(img.at(TILES, t - 3)):
                        act.wait_ge(added, img.at(TILES, t - 3))
                    nc.scalar.activation(shiftb[:, t % 4, :], w_row[:, img.slot, :], ACT.Copy, scale=s)
                    if comes(img.at(TILES, t - 1)):
                        act.wait_ge(scaled, img.at(TILES, t - 1))
                    nc.scalar.activation(gain_ps[t % 2][:], u_row[:, img.slot, :], ACT.Identity, scale=s,
                                         bias=1.0).then_inc(gain_done, 1)

            def gate_exps(img, k):
                act.wait_ge(t_dotted, img.at(TILES, (k + 1) * CHUNK))
                c = slice(k * CHUNK, (k + 1) * CHUNK)
                nc.scalar.activation(texp[:, c], tdot[:, c], ACT.Exp, scale=-1.0, bias=shift[:]
                                     ).then_inc(gate_exp, 1)

            def stats(img):
                act.wait_ge(ev["stat_ps"], img.b + 1)
                nc.scalar.activation(partial[:], sum_ps[:], ACT.Copy).then_inc(ev["sum_copied"], 1)

            def phase(prev, cur, nxt):
                if prev:
                    gains(prev, 8, 11)
                act.wait_ge(ev["max_neg"], cur.b + 1)
                nc.scalar.activation(prob[:], logit[:], ACT.Exp, bias=neg_max[:], accum_out=mass[:]
                                     ).then_inc(ev["probs"], 1)
                if prev:
                    gate_exps(prev, 2)
                    gains(prev, 11, 17)
                    gate_exps(prev, 3)
                act.wait_ge(ev["weighted_ps"], cur.b + 1)
                nc.scalar.activation(partial[:], weighted_ps[:], ACT.Copy).then_inc(ev["weighted"], 1)
                if prev:
                    gains(prev, 17, 26)
                act.wait_ge(ev["z_beta"], cur.b + 1)
                nc.scalar.activation(zexp[:], zbet[:], ACT.Exp, scale=-1.0).then_inc(ev["z_exp"], 1)
                if prev:
                    gains(prev, 26, 28)
                act.wait_ge(ev["q_max"], cur.b + 1)
                nc.scalar.activation(arow[:], qrow[:], ACT.Exp, bias=qmax[:], accum_out=asum[:]
                                     ).then_inc(ev["q_exp"], 1)
                act.wait_ge(ev["u_ps"], cur.b + 1)
                nc.scalar.activation(u_row[:, cur.slot, :], weighted_ps[:], ACT.Copy).then_inc(ev["u_row"], 1)
                if prev:
                    gains(prev, 28, 30)
                act.wait_ge(ev["w_ps"], cur.b + 1)
                nc.scalar.activation(w_row[:, cur.slot, :], weighted_ps[:], ACT.Copy).then_inc(ev["w_row"], 1)
                if prev:
                    gains(prev, 30, 32)
                act.wait_ge(ev["shift"], cur.b + 1)
                gate_exps(cur, 0)
                gains(cur, 0, 2)
                gate_exps(cur, 1)
                gains(cur, 2, 7)
                if nxt:
                    stats(nxt)
                gains(cur, 7, 8)

            stats(image(0, 0))
            phases(act, phase)
            gains(LAST, 8, 11)
            gate_exps(LAST, 2)
            gains(LAST, 11, 15)
            gate_exps(LAST, 3)
            gains(LAST, 15, 32)

        @block.tensor
        def _(pe):
            pe.wait_ge(made, CONSTS + 1)

            def gram(img, lo, hi):
                for t in range(lo, hi):
                    if t % QUAD == 0:
                        pe.wait_ge(loaded[img.slot][t // QUAD], img.use * 16 + 16)
                    if t == 0:
                        if comes(img.at(1, 0)):
                            pe.wait_ge(ev["square_col"], img.at(1, 0))
                        if comes(img.at(1, 0)):
                            pe.wait_ge(ev["sum_copied"], img.at(1, 0))
                    tile = xs[:, img.slot, t, :]
                    s = (t % STRIPS) * SW
                    nc.tensor.matmul(sum_ps[s:s + SW, :], ones[:, 0:SW], tile, start=t < STRIPS,
                                     stop=t >= TILES - STRIPS)
                    for j in range(J):
                        cols = slice(j * P, (j + 1) * P)
                        last = nc.tensor.matmul(gram_ps[:, cols], tile[:, cols], tile[:, cols],
                                                start=t == 0 and j == 0, stop=t == TILES - 1 and j == J - 1,
                                                skip_group_check=True)
                    if t == TILES - 1:
                        last.then_inc(ev["stat_ps"], 1)

            def row(dst, column_diag):
                return nc.tensor.matmul(dst[:], ones[:], column_diag[:].rearrange("p j c -> p (j c)"),
                                        start=True, stop=True)

            def stats(img):
                pe.wait_ge(ev["sum_copied"], img.b + 1)
                for j in range(J):
                    last = nc.tensor.matmul(small[:, j:j + 1], partial[:, j * P:(j + 1) * P], sel[:, 0:1],
                                            start=True, stop=True)
                last.then_inc(ev["stat_group_ps"], 1)
                pe.wait_ge(ev["stat_mean"], img.b + 1)
                pe.wait_ge(ev["square_col"], img.b + 1)
                nc.tensor.matmul(small[:, 8:8 + 2 * J], block16[:], stat[:, img.slot, :], start=True,
                                        stop=True).then_inc(ev["stat_group"], 1)
                pe.wait_ge(ev["mwq_col"], img.b + 1)
                nc.tensor.matmul(small[:, 16:17], ones[:], mwq_sum[:], start=True, stop=True)
                pe.wait_ge(ev["wq_diag"], img.b + 1)
                row(wq_ps, diag).then_inc(ev["wq_row"], 1)

            def softmax(cur):
                pe.wait_ge(ev["logits_max"], cur.b + 1)
                nc.tensor.transpose(small[0:1, P:2 * P], lmax[:], ident[:]).then_inc(ev["max_t"], 1)
                pe.wait_ge(ev["max_one"], cur.b + 1)
                nc.tensor.matmul(small[:, 17:18], neg_row[:], one_max[:], start=True, stop=True).then_inc(ev["max_ps"], 1)
                pe.wait_ge(ev["probs"], cur.b + 1)
                nc.tensor.matmul(small[:, 18:19], ones[:], mass[:], start=True, stop=True).then_inc(ev["mass_ps"], 1)
                for t in range(TILES):
                    s = (t % STRIPS) * SW
                    last = nc.tensor.matmul(weighted_ps[s:s + SW, :], prob[:, t:t + 1].to_broadcast([P, SW]),
                                            xs[:, cur.slot, t, :], start=t < STRIPS, stop=t >= TILES - STRIPS)
                last.then_inc(ev["weighted_ps"], 1)

            def columns(dst, weight, rhs, blocks, depth):
                for o in range(blocks):
                    for i in range(depth):
                        last = nc.tensor.matmul(dst[:, o:o + 1], weight[:, i, o * P:(o + 1) * P], rhs[:, i:i + 1],
                                                start=i == 0, stop=i == depth - 1)
                return last

            def channel(cur, fill):
                fill(8, 9)
                pe.wait_ge(ev["weighted"], cur.b + 1)
                pe.wait_ge(ev["mass_inv"], cur.b + 1)
                for j in range(J):
                    last = nc.tensor.matmul(small[:, 20 + j:21 + j], partial[:, j * P:(j + 1) * P],
                                            sel[:, 1:2], start=True, stop=True)
                last.then_inc(ev["pooled_ps"], 1)
                fill(9, 10)
                pe.wait_ge(ev["pooled"], cur.b + 1)
                columns(small[:, 28:28 + J], wvz, pool_y, J, J).then_inc(ev["z_ps"], 1)
                fill(10, 11)
                pe.wait_ge(ev["z_sq"], cur.b + 1)
                nc.tensor.matmul(small[:, 36:37], ones[:], zsq[:], start=True, stop=True
                                 ).then_inc(ev["z_var_ps"], 1)
                fill(11, 13)

            def spatial(cur, fill):
                pe.wait_ge(ev["y_mean"], cur.b + 1)
                for j in range(J):
                    last = nc.tensor.matmul(small[0:1, D:2 * D], ymean[:, j:j + 1], wq2[:, j, :], start=j == 0,
                                            stop=j == J - 1)
                last.then_inc(ev["q_ps"], 1)
                pe.wait_ge(ev["u_diag"], cur.b + 1)
                row(weighted_ps, diag).then_inc(ev["u_ps"], 1)
                fill(13, 14)
                pe.wait_ge(ev["q_inv"], cur.b + 1)
                for h in range(H):
                    last = nc.tensor.matmul(small[:, 40 + h:41 + h], arow[:, h * P:(h + 1) * P], ainv[:],
                                            start=True, stop=True)
                last.then_inc(ev["a_ps"], 1)
                pe.wait_ge(ev["w_diag"], cur.b + 1)
                pe.wait_ge(ev["u_row"], cur.b + 1)
                row(weighted_ps, diag).then_inc(ev["w_ps"], 1)
                pe.wait_ge(ev["a"], cur.b + 1)
                columns(small[:, 44:44 + J], wv2t, acol, J, H).then_inc(ev["k_ps"], 1)
                fill(14, 15)
                pe.wait_ge(ev["v_diag"], cur.b + 1)
                row(v_ps, diag).then_inc(ev["v_row"], 1)
                pe.wait_ge(ev["shift_b"], cur.b + 1)
                nc.tensor.matmul(small[:, 48:49], ones[:], vm_ab[:], start=True, stop=True
                                 ).then_inc(ev["shift_ps"], 1)

            def phase(prev, cur, nxt):
                def fill(lo, hi):
                    if nxt:
                        gram(nxt, lo, hi)

                fill(0, 8)
                softmax(cur)
                channel(cur, fill)
                spatial(cur, fill)
                fill(15, TILES)
                if nxt:
                    stats(nxt)

            gram(image(0, 0), 0, TILES)
            stats(image(0, 0))
            pe.wait_ge(weights_in, 16 * 2)
            pe.wait_ge(vectors_in, 16 * 8)
            for j in range(J):
                if j >= 2:
                    pe.wait_ge(product, j - 1)
                for h in range(H):
                    last = nc.tensor.matmul(gain_ps[j % 2][:], wv_t[:, h, j * P:(j + 1) * P], wz[:, h, :],
                                            start=h == 0, stop=h == H - 1)
                last.then_inc(product_ps, 1)
            columns(small[:, 52:52 + J], wz, bv_col, J, H).then_inc(bias_ps, 1)
            pe.wait_ge(bias, 2)
            nc.tensor.matmul(small[:, 56:57], ones[:], bvz_sum[:], start=True, stop=True).then_inc(bias_ps, 1)
            pe.wait_ge(spatial_in, 16 * 2)
            phases(pe, phase)

        @block.vector
        def _(dve):
            v = nc.vector
            dve.wait_ge(made, CONSTS + 1)
            dve.wait_ge(vectors_in, 16 * 8)
            v.tensor_scalar(bq_part[:], bq[:], 1.0 / P, None, ALU.mult).then_inc(bq_parted, 1)
            dve.wait_ge(bq_parted, 1)

            def dots(img, lo, hi, row_ps, dst, junk, dotted):
                for t in range(lo, hi):
                    if comes(img.at(TILES, t - 1)):
                        dve.wait_ge(dotted, img.at(TILES, t - 1))
                    v.tensor_tensor_reduce(out=junk[:, t % 2, :], in0=xs[:, img.slot, t, :], in1=row_ps[:],
                                           scale=1.0, scalar=0.0, op0=ALU.mult, op1=ALU.add,
                                           accum_out=dst[:, t:t + 1]).then_inc(dotted, 1)

            def q_dots(img, lo, hi):
                dots(img, lo, hi, wq_ps, qdot, q_junk, q_dotted)

            def gate_dots(img, lo, hi):
                dots(img, lo, hi, v_ps, tdot, t_junk, t_dotted)

            def gates(img, k):
                c = slice(k * CHUNK, (k + 1) * CHUNK)
                dve.wait_ge(gate_exp, img.at(CHUNKS, k + 1))
                v.tensor_scalar(tden[:, c], texp[:, c], 1.0, None, ALU.add).then_inc(gate_den, 1)
                dve.wait_ge(gate_den, img.at(CHUNKS, k + 1))
                v.reciprocal(gate[:, img.slot, c], tden[:, c]).then_inc(gate_done, 1)

            def scale(img, lo, hi):
                for t in range(lo, hi):
                    k, r = t // CHUNK, t % CHUNK
                    if r == 0:
                        if comes(img.at(16 * CHUNKS // 2, 16 * (k // 2))):
                            dve.wait_ge(stored[k % 2], img.at(16 * CHUNKS // 2, 16 * (k // 2)))
                    dve.wait_ge(gain_done, img.at(TILES, t + 1))
                    v.tensor_tensor(stage[:, k % 2, r, :], xs[:, img.slot, t, :], gain_ps[t % 2][:],
                                    ALU.mult).then_inc(scaled, 1)

            def diagonal(column, img, name):
                ins = v.tensor_tensor(diag[:], ident[:].unsqueeze(1).to_broadcast([P, J, P]),
                                      column.unsqueeze(2).to_broadcast([P, J, P]), ALU.mult)
                ins.then_inc(ev[name], 1)

            def stats(img, fill):
                dve.wait_ge(ev["stat_ps"], img.b + 1)
                for j in range(J):
                    last = v.tensor_tensor_reduce(out=diag[:, j, :],
                                                  in0=gram_ps[:, j * P:(j + 1) * P], in1=ident[:],
                                                  scale=1.0 / TOKENS, scalar=0.0, op0=ALU.mult, op1=ALU.add,
                                                  accum_out=stat[:, img.slot, J + j:J + j + 1])
                last.then_inc(ev["square_col"], 1)
                dve.wait_ge(ev["square_col"], img.b + 1)
                dve.wait_ge(ev["stat_group_ps"], img.b + 1)
                v.tensor_copy(stat[:, img.slot, 0:J], small[:, 0:J]).then_inc(ev["stat_mean"], 1)
                fill(5, 6)
                dve.wait_ge(ev["stat_group"], img.b + 1)
                g = gstat[:, img.slot, :]
                v.tensor_copy(g, small[:, 8:8 + 2 * J]).then_inc(ev["stat_group_sb"], 1)
                dve.wait_ge(ev["stat_group_sb"], img.b + 1)
                v.tensor_tensor(m2[:], g[:, 0:J], g[:, 0:J], ALU.mult).then_inc(ev["stat_m2"], 1)
                dve.wait_ge(ev["stat_m2"], img.b + 1)
                v.scalar_tensor_tensor(out=var[:], in0=g[:, J:2 * J], scalar=GN_EPS, in1=m2[:], op0=ALU.add,
                                            op1=ALU.subtract).then_inc(ev["stat_var"], 1)
                dve.wait_ge(ev["stat_var"], img.b + 1)
                fill(6, 7)
                dve.wait_ge(ev["rs"], img.b + 1)
                v.tensor_tensor(wqs[:], wq_col[:], rs[:, img.slot, :], ALU.mult).then_inc(ev["wq_col"], 1)
                dve.wait_ge(ev["wq_col"], img.b + 1)
                diagonal(wqs[:], img, "wq_diag")
                v.tensor_tensor_reduce(out=mwq[:], in0=g[:, 0:J], in1=wqs[:], scale=-1.0, scalar=bq_part[:],
                                       op0=ALU.mult, op1=ALU.add, accum_out=mwq_sum[:]
                                       ).then_inc(ev["mwq_col"], 1)
                fill(7, 8)

            def phase(prev, cur, nxt):
                def fill_prev(lo, hi):
                    if prev:
                        scale(prev, lo, hi)

                m = gstat[:, cur.slot, 0:J]
                r = rs[:, cur.slot, :]
                dve.wait_ge(ev["wq_row"], cur.b + 1)
                q_dots(cur, 0, TILES)
                dve.wait_ge(q_dotted, cur.at(TILES, TILES))
                v.tensor_scalar(logit[:], qdot[:], small[:, 16:17], None, ALU.add, ALU.max,
                                     accum_out=lmax[:]).then_inc(ev["logits_max"], 1)
                dve.wait_ge(ev["logits_max"], cur.b + 1)
                fill_prev(8, 9)
                if prev:
                    gate_dots(prev, 20, 21)
                dve.wait_ge(ev["max_t"], cur.b + 1)
                v.tensor_reduce(one_max[:], small[0:1, P:2 * P], AX.X, ALU.max).then_inc(ev["max_one"], 1)
                if prev:
                    gate_dots(prev, 21, 22)
                dve.wait_ge(ev["max_ps"], cur.b + 1)
                v.tensor_copy(neg_max[:], small[:, 17:18]).then_inc(ev["max_neg"], 1)
                if prev:
                    gate_dots(prev, 22, 24)
                    for n in range(2):
                        scale(prev, 9 + n, 10 + n)
                        gate_dots(prev, 24 + n, 25 + n)
                dve.wait_ge(ev["mass_ps"], cur.b + 1)
                v.reciprocal(inv_mass[:], small[:, 18:19]).then_inc(ev["mass_inv"], 1)
                if prev:
                    gates(prev, 2)
                    for n in range(2, 7):
                        scale(prev, 9 + n, 10 + n)
                        gate_dots(prev, 24 + n, 25 + n)
                    gate_dots(prev, 31, 32)
                    scale(prev, 16, 17)
                    gates(prev, 3)
                    scale(prev, 17, 18)
                dve.wait_ge(ev["pooled_ps"], cur.b + 1)
                dve.wait_ge(ev["mass_inv"], cur.b + 1)
                v.scalar_tensor_tensor(out=pool_n[:], in0=small[:, 20:20 + J], scalar=inv_mass[:], in1=m,
                                       op0=ALU.mult, op1=ALU.subtract).then_inc(ev["pooled_n"], 1)
                dve.wait_ge(ev["pooled_n"], cur.b + 1)
                v.tensor_tensor(pool_y[:], pool_n[:], r, ALU.mult).then_inc(ev["pooled"], 1)
                v.tensor_tensor(ycent[:], stat[:, cur.slot, 0:J], m, ALU.subtract).then_inc(ev["y_cent"], 1)
                fill_prev(18, 21)
                dve.wait_ge(ev["z_ps"], cur.b + 1)
                v.tensor_tensor(zcent[:], small[:, 28:28 + J], bvz[:], ALU.add).then_inc(ev["z"], 1)
                dve.wait_ge(ev["z"], cur.b + 1)
                v.tensor_tensor_reduce(out=zjunk[:], in0=zcent[:], in1=zcent[:], scale=1.0 / C, scalar=0.0,
                                       op0=ALU.mult, op1=ALU.add, accum_out=zsq[:]).then_inc(ev["z_sq"], 1)
                v.tensor_tensor(zgam[:], zcent[:], gamma[:], ALU.mult).then_inc(ev["z_gamma"], 1)
                fill_prev(21, 22)
                dve.wait_ge(ev["z_var_ps"], cur.b + 1)
                v.tensor_scalar(zvar[:], small[:, 36:37], LN_EPS, None, ALU.add).then_inc(ev["z_var"], 1)
                fill_prev(22, 23)
                dve.wait_ge(ev["z_gamma"], cur.b + 1)
                dve.wait_ge(ev["z_rstd"], cur.b + 1)
                v.scalar_tensor_tensor(out=zbet[:], in0=zgam[:], scalar=zrstd[:], in1=beta[:], op0=ALU.mult,
                                       op1=ALU.add).then_inc(ev["z_beta"], 1)
                fill_prev(23, 24)
                dve.wait_ge(ev["z_exp"], cur.b + 1)
                v.tensor_scalar(zden[:], zexp[:], 1.0, None, ALU.add).then_inc(ev["z_den"], 1)
                dve.wait_ge(ev["z_den"], cur.b + 1)
                v.reciprocal(cw[:], zden[:]).then_inc(ev["cw"], 1)
                dve.wait_ge(ev["cw"], cur.b + 1)
                v.tensor_tensor(ucol[:], cw[:], r, ALU.mult).then_inc(ev["u"], 1)
                dve.wait_ge(ev["u"], cur.b + 1)
                v.tensor_tensor(ymean[:], ycent[:], ucol[:], ALU.mult).then_inc(ev["y_mean"], 1)
                diagonal(ucol[:], cur, "u_diag")
                v.scalar_tensor_tensor(out=wcol[:], in0=ucol[:], scalar=-1.0, in1=m, op0=ALU.mult,
                                       op1=ALU.mult).then_inc(ev["w"], 1)
                fill_prev(24, 26)
                dve.wait_ge(ev["q_ps"], cur.b + 1)
                v.tensor_tensor(qrow[:], small[0:1, D:2 * D], bq2_row[:], ALU.add).then_inc(ev["q_row"], 1)
                dve.wait_ge(ev["q_row"], cur.b + 1)
                v.tensor_reduce(qmax[:], qrow[:], AX.X, ALU.max, negate=True).then_inc(ev["q_max"], 1)
                fill_prev(26, 27)
                dve.wait_ge(ev["q_exp"], cur.b + 1)
                v.reciprocal(ainv[:], asum[:]).then_inc(ev["q_inv"], 1)
                dve.wait_ge(ev["w"], cur.b + 1)
                dve.wait_ge(ev["u_ps"], cur.b + 1)
                diagonal(wcol[:], cur, "w_diag")
                fill_prev(27, 28)
                dve.wait_ge(ev["a_ps"], cur.b + 1)
                v.tensor_copy(acol[:], small[:, 40:40 + H]).then_inc(ev["a"], 1)
                dve.wait_ge(ev["a"], cur.b + 1)
                fill_prev(28, 30)
                dve.wait_ge(ev["k_ps"], cur.b + 1)
                v.tensor_tensor(kcol[:], small[:, 44:44 + J], ucol[:], ALU.mult).then_inc(ev["v_col"], 1)
                dve.wait_ge(ev["v_col"], cur.b + 1)
                dve.wait_ge(ev["w_ps"], cur.b + 1)
                diagonal(kcol[:], cur, "v_diag")
                v.tensor_tensor_reduce(out=terms[:], in0=kcol[:], in1=m, scale=1.0, scalar=0.0, op0=ALU.mult,
                                       op1=ALU.add, accum_out=vm[:]).then_inc(ev["shift_a"], 1)
                dve.wait_ge(ev["shift_a"], cur.b + 1)
                v.tensor_tensor_reduce(out=terms[:, 0:H], in0=acol[:], in1=bv2_col[:], scale=-1.0, scalar=vm[:],
                                       op0=ALU.mult, op1=ALU.add, accum_out=vm_ab[:]
                                       ).then_inc(ev["shift_b"], 1)
                fill_prev(30, 32)
                dve.wait_ge(ev["shift_ps"], cur.b + 1)
                v.tensor_copy(shift[:], small[:, 48:49]).then_inc(ev["shift"], 1)
                dve.wait_ge(ev["v_row"], cur.b + 1)
                gate_dots(cur, 0, 12)
                gates(cur, 0)
                gate_dots(cur, 12, 16)
                scale(cur, 0, 1)
                gate_dots(cur, 16, 17)
                scale(cur, 1, 2)
                gates(cur, 1)
                for n in range(3):
                    gate_dots(cur, 17 + n, 18 + n)
                    scale(cur, 2 + n, 3 + n)
                if nxt:
                    stats(nxt, lambda lo, hi: scale(cur, lo, hi))
                else:
                    scale(cur, 5, 8)

            stats(image(0, 0), lambda lo, hi: None)
            for j in range(J):
                dve.wait_ge(product_ps, j + 1)
                v.tensor_reduce(wvz_sum[:, j:j + 1], gain_ps[j % 2][:], AX.X, ALU.add).then_inc(product_sum, 1)
                dve.wait_ge(product_sum, j + 1)
                v.tensor_scalar(wvz_mean[:, j:j + 1], wvz_sum[:, j:j + 1], 1.0 / C, None, ALU.mult
                                ).then_inc(product_mean, 1)
                dve.wait_ge(product_mean, j + 1)
                v.tensor_scalar(wvz[:, j, :], gain_ps[j % 2][:], wvz_mean[:, j:j + 1], None, ALU.subtract
                                ).then_inc(product, 1)
            dve.wait_ge(bias_ps, 1)
            v.tensor_tensor(bvz[:], small[:, 52:52 + J], bz_col[:], ALU.add).then_inc(bias, 1)
            dve.wait_ge(bias, 1)
            v.tensor_reduce(bvz_sum[:], bvz[:], AX.X, ALU.add).then_inc(bias, 1)
            dve.wait_ge(bias_ps, 2)
            v.tensor_scalar(bvz_mean[:], small[:, 56:57], 1.0 / C, None, ALU.mult).then_inc(bias, 1)
            dve.wait_ge(bias, 3)
            v.tensor_scalar(bvz[:], bvz[:], bvz_mean[:], None, ALU.subtract).then_inc(bias, 1)
            dve.wait_ge(bias, 4)
            phases(dve, phase)
            scale(LAST, 8, 9)
            gate_dots(LAST, 20, 24)
            scale(LAST, 9, 10)
            gate_dots(LAST, 24, 28)
            gates(LAST, 2)
            scale(LAST, 10, 12)
            gate_dots(LAST, 28, 32)
            scale(LAST, 12, 14)
            gates(LAST, 3)
            scale(LAST, 14, 32)


def kernel(**inputs):
    import numpy as np
    import concourse.bacc as bacc
    from concourse.bass_utils import run_bass_kernel_spmd as run

    nc = bacc.Bacc("TRN2", target_bir_lowering=False, num_devices=1)
    arrays = {"x": np.ascontiguousarray(inputs["x"])}
    for name in ("ch_wv_b", "ch_wq_w", "ch_wq_b", "ch_wz_w", "ch_wz_b", "ln_gamma", "ln_beta",
                 "sp_wv_b", "sp_wq_w", "sp_wq_b"):
        arrays[name] = np.ascontiguousarray(inputs[f"L0_conv_{name}"])
    for name in ("ch_wq_w", "ch_wv_b", "ch_wz_b", "ln_gamma", "ln_beta", "sp_wv_b"):
        arrays[name] = np.ascontiguousarray(np.transpose(np.reshape(arrays[name], (-1, P))))
    for name in ("ch_wv_w", "sp_wv_w"):
        arrays[f"{name}_t"] = np.ascontiguousarray(np.transpose(inputs[f"L0_conv_{name}"]))
    w = {name: nc.dram_tensor(name, a.shape, mybir.dt.from_np(a.dtype), kind="ExternalInput").ap()
         for name, a in arrays.items()}
    out = nc.dram_tensor("out", arrays["x"].shape, F32, kind="ExternalOutput").ap()
    build(nc, w["x"], w, out)
    return run(nc, [arrays], core_ids=[0]).results[0]["out"]
```

```python
from contextlib import ExitStack

import concourse.bass as bass
from concourse import mybir

F32 = mybir.dt.float32
BF16 = mybir.dt.bfloat16
ALU = mybir.AluOpType
ACT = mybir.ActivationFunctionType
AX = mybir.AxisListType

P = 128
IMAGES, TOKENS, C = 16, 64 * 64, 512
TILES = TOKENS // P
J = C // P
D = C // 2
H = D // P
GROUP = 16
CHUNK = 8
QUAD = 4
QUADS = TILES // QUAD
CHUNKS = TILES // CHUNK
PART = 16
PARTS = (0, PART, TILES)
SHARED = 6
DVE_DOTS = TILES - SHARED
GATE_FIRST, GATE_SHARED = 12, 4
STRIPS = 4
SW = P // STRIPS
GN_EPS, LN_EPS = 1e-5, 1e-3

EVENTS = (
    "sum_copied", "square_col", "stat_ps", "stat_mean", "stat_group_ps", "stat_group", "stat_group_sb", "stat_m2",
    "stat_var", "rs", "wq_col", "mwq_col", "wq_diag", "wq_row", "wq_copied",
    "max_lower", "factor", "mass_ps", "mass_sum", "mass_inv", "part_weight", "pooled_a", "pooled_n", "pooled",
    "z_row_ps", "z_row", "z_ps", "z", "z_sq", "z_var_ps", "z_var", "z_rstd", "z_gamma", "z_beta", "z_exp", "z_den",
    "cw", "u", "w",
    "y_cent", "y_mean", "q_ps", "q_row", "q_max", "q_exp", "q_inv", "a_ps", "a", "k_ps", "a_bias",
    "shift", "v_row", "v_copied", "u_diag", "u_ps", "u_row", "w_diag", "w_ps",
    "w_row",
)

PART_EVENTS = ("logits_max", "max_t", "max_one", "max_ps", "max_neg", "probs", "weighted_ps", "weighted", "pooled_ps")


class Image:

    def __init__(self, b, slot, use):
        self.b, self.slot, self.use = b, slot, use

    def at(self, count, n):
        return self.b * count + n


def comes(value):
    return not isinstance(value, int) or value > 0


def dve_gate_dots(tiles):
    return tiles - min(max(tiles - GATE_FIRST, 0), GATE_SHARED)


def image(i, off):
    return Image(i * 2 + off, off % 2, i + off // 2)


def build(nc, x, w, out):
    ctx = ExitStack()
    with ctx:
        def sb(name, shape, dt=F32):
            return ctx.enter_context(nc.sbuf_tensor(name, shape, dt))

        def sem(name):
            return ctx.enter_context(nc.semaphore(name))

        xs = sb("xs", [P, 2, TILES, C])
        stage = sb("stage", [P, 2, CHUNK, C])
        shiftb = sb("shiftb", [P, 4, C])
        q_junk = sb("q_junk", [P, 2, C], BF16)
        t_junk = sb("t_junk", [P, 2, C], BF16)
        partial = sb("partial", [P, C])
        diag = sb("diag", [P, J, P])
        u_row = sb("u_row", [P, 2, C])
        w_row = sb("w_row", [P, 2, C])
        wvz = sb("wvz", [P, J, C])
        wvz_sum = sb("wvz_sum", [P, J])
        wvz_mean = sb("wvz_mean", [P, J])
        wq2 = sb("wq2", [P, J, D])
        wv2t = sb("wv2t", [P, H, C])
        ident = sb("ident", [P, P])
        ones = sb("ones", [P, P])
        block16 = sb("block16", [P, P])
        sel = sb("sel", [P, 2])
        wq_col = sb("wq_col", [P, J])
        bv_col = sb("bv_col", [P, H])
        bz_col = sb("bz_col", [P, J])
        gamma = sb("gamma", [P, J])
        beta = sb("beta", [P, J])
        bv2_col = sb("bv2_col", [P, H])
        bq2_row = sb("bq2_row", [1, D])
        bq = sb("bq", [P, 1])
        bq_part = sb("bq_part", [P, 1])
        stat = sb("stat", [P, 2, 2 * J])
        gstat = sb("gstat", [P, 2, 2 * J])
        m2 = sb("m2", [P, J])
        var = sb("var", [P, J])
        rs = sb("rs", [P, 2, J])
        wqs = sb("wqs", [P, J])
        mwq = sb("mwq", [P, J])
        mwq_sum = sb("mwq_sum", [P, 1])
        qdot = sb("qdot", [P, TILES])
        logit = sb("logit", [P, TILES])
        lmax = sb("lmax", [P, 2])
        one_max = sb("one_max", [1, 1])
        neg_row = sb("neg_row", [1, P])
        neg_max = sb("neg_max", [P, 2])
        neg_all = sb("neg_all", [P, 1])
        factor = sb("factor", [P, 2])
        part_weight = sb("part_weight", [P, 2])
        mass_junk = sb("mass_junk", [P, 2])
        mass_sum = sb("mass_sum", [P, 1])
        prob = sb("prob", [P, TILES])
        mass = sb("mass", [P, 2])
        inv_mass = sb("inv_mass", [P, 1])
        pool_a = sb("pool_a", [P, J])
        pool_n = sb("pool_n", [P, J])
        pool_y = sb("pool_y", [P, J])
        bvz = sb("bvz", [P, J])
        bvz_sum = sb("bvz_sum", [P, 1])
        bvz_mean = sb("bvz_mean", [P, 1])
        zcent = sb("zcent", [P, J])
        zjunk = sb("zjunk", [P, J])
        zsq = sb("zsq", [P, 1])
        zvar = sb("zvar", [P, 1])
        zrstd = sb("zrstd", [P, 1])
        zgam = sb("zgam", [P, J])
        zbet = sb("zbet", [P, J])
        zexp = sb("zexp", [P, J])
        zden = sb("zden", [P, J])
        cw = sb("cw", [P, J])
        ucol = sb("ucol", [P, J])
        wcol = sb("wcol", [P, J])
        ycent = sb("ycent", [P, J])
        ymean = sb("ymean", [P, J])
        qrow = sb("qrow", [1, D])
        qmax = sb("qmax", [1, 1])
        asum = sb("asum", [1, 1])
        ainv = sb("ainv", [1, 1])
        acol = sb("acol", [P, H])
        a_bias = sb("a_bias", [P, 1])
        shift = sb("shift", [P, 1])
        tdot = sb("tdot", [P, TILES])
        texp = sb("texp", [P, TILES])
        tden = sb("tden", [P, TILES])
        gate = sb("gate", [P, 2, TILES])
        halves = sb("halves", [P, J])

        def bank(name):
            return ctx.enter_context(nc.psum_tensor(name, [P, C], F32))

        gram_ps = bank("gram_ps")
        sum_ps = bank("sum_ps")
        weighted_ps = bank("weighted_ps")
        wq_ps = bank("wq_ps")
        v_ps = bank("v_ps")
        small = bank("small")
        part_ps = (weighted_ps, wq_ps)
        part_sums = (diag[:].rearrange("p j c -> p (j c)"), partial[:])
        w_diag = partial[:].rearrange("p (j c) -> p j c", c=P)
        gain_ps = [bank("gain0"), bank("gain1")]

        ev = {name: sem(name) for name in EVENTS + PART_EVENTS}
        loaded = [[sem(f"loaded_{s}_{k}") for k in range(QUADS)] for s in range(2)]
        stored = [sem(f"stored_{s}") for s in range(2)]
        vectors_in = sem("vectors_in")
        weights_in = sem("weights_in")
        spatial_in = sem("spatial_in")
        product_ps = sem("product_ps")
        product_sum = sem("product_sum")
        product_mean = sem("product_mean")
        product = sem("product")
        bias_ps = sem("bias_ps")
        bias = sem("bias")
        bq_parted = sem("bq_parted")
        made = sem("made")
        q_dotted = sem("q_dotted")
        q_product = sem("q_product")
        q_summed = sem("q_summed")
        t_dotted = sem("t_dotted")
        t_product = sem("t_product")
        t_summed = sem("t_summed")
        gate_exp = sem("gate_exp")
        gate_den = sem("gate_den")
        gate_done = sem("gate_done")
        gain_done = sem("gain_done")
        scaled = sem("scaled")
        added = sem("added")

        CONSTS = 9

        xv = x.rearrange("b h w c -> b (h w) c").rearrange("b (p t) c -> b p t c", p=P)
        ov = out.rearrange("b h w c -> b (h w) c").rearrange("b (p t) c -> b p t c", p=P)

        wv_t = stage[:, 0, 0:H, :]
        wz = stage[:, 0, H:2 * H, :]

        block = ctx.enter_context(nc.Block())

        def phases(engine, phase):
            phase(None, image(0, 0), image(0, 1))
            with engine.Fori(0, (IMAGES - 2) // 2) as i:
                phase(image(i, 0), image(i, 1), image(i, 2))
                phase(image(i, 1), image(i, 2), image(i, 3))
            last = IMAGES - 1
            phase(image(last // 2, 0), image(last // 2, 1), None)

        LAST = image((IMAGES - 1) // 2, 1)

        @block.sync
        def _(sp):
            def load(img, q):
                tiles = slice(q * QUAD, (q + 1) * QUAD)
                if not (isinstance(img.b, int) and img.b < 2):
                    sp.wait_ge(scaled, img.at(TILES, QUAD * (q + 1) - 2 * TILES))
                sp.dma_start(xs[:, img.slot, tiles, :],
                             xv[bass.ds(img.b, 1), :, tiles, :].rearrange("o p t c -> (o p) t c")
                             ).then_inc(loaded[img.slot][q], 16)

            def store(img, k):
                sp.wait_ge(added, img.at(TILES, (k + 1) * CHUNK))
                sp.dma_start(ov[bass.ds(img.b, 1), :, k * CHUNK:(k + 1) * CHUNK, :].rearrange("o p t c -> (o p) t c"),
                             stage[:, k % 2, :, :]).then_inc(stored[k % 2], 16)

            def phase(prev, cur, nxt):
                def loads(lo, hi):
                    if nxt:
                        for q in range(lo, hi):
                            load(nxt, q)

                def stores(lo, hi):
                    if prev:
                        for k in range(lo, hi):
                            store(prev, k)

                loads(0, 4)
                stores(0, 2)
                loads(4, 6)
                stores(2, 3)
                loads(6, 8)
                stores(3, 4)

            for dst, src in ((wq_col, w["ch_wq_w"]), (bv_col, w["ch_wv_b"]), (bz_col, w["ch_wz_b"]),
                             (gamma, w["ln_gamma"]), (beta, w["ln_beta"]), (bv2_col, w["sp_wv_b"]),
                             (bq2_row, w["sp_wq_b"].rearrange("(o d) -> o d", o=1)),
                             (bq, w["ch_wq_b"].rearrange("(o d) -> o d", o=1).to_broadcast([P, 1]))):
                sp.dma_start(dst[:], src).then_inc(vectors_in, 16)
            for q in range(QUADS):
                load(image(0, 0), q)
            sp.dma_start(wv_t, w["ch_wv_w_t"].rearrange("(h p) c -> p h c", p=P)).then_inc(weights_in, 16)
            sp.dma_start(wz, w["ch_wz_w"].rearrange("(h p) c -> p h c", p=P)).then_inc(weights_in, 16)
            sp.dma_start(wq2[:], w["sp_wq_w"].rearrange("(j p) d -> p j d", p=P)).then_inc(spatial_in, 16)
            sp.dma_start(wv2t[:], w["sp_wv_w_t"].rearrange("(h p) c -> p h c", p=P)).then_inc(spatial_in, 16)
            phases(sp, phase)
            for k in range(CHUNKS):
                store(LAST, k)
            for s in range(2):
                sp.wait_ge(stored[s], 16 * IMAGES * CHUNKS // 2)

        @block.gpsimd
        def _(pool):
            nc.gpsimd.memset(ident[:], 0.0).then_inc(made, 1)
            nc.gpsimd.memset(ones[:], 1.0).then_inc(made, 1)
            nc.gpsimd.memset(block16[:], 1.0 / GROUP).then_inc(made, 1)
            nc.gpsimd.memset(sel[:, 0:1], 1.0 / (SW * TOKENS)).then_inc(made, 1)
            nc.gpsimd.memset(sel[:, 1:2], 1.0 / SW).then_inc(made, 1)
            nc.gpsimd.memset(neg_row[:], -1.0).then_inc(made, 1)
            nc.gpsimd.memset(halves[:], -0.5).then_inc(made, 1)
            pool.wait_ge(made, 7)
            nc.gpsimd.affine_select(out=ident[:], in_=ident[:], compare_op=ALU.not_equal, fill=1.0, base=0,
                                    pattern=[[-1, P]], channel_multiplier=1).then_inc(made, 1)
            blocks = block16[:].rearrange("p (g e) -> p g e", e=GROUP)
            nc.gpsimd.affine_select(out=blocks, in_=blocks, compare_op=ALU.is_ge, fill=0.0, base=0,
                                    pattern=[[-GROUP, P // GROUP], [0, GROUP]], channel_multiplier=1
                                    ).then_inc(made, 1)
            pool.wait_ge(made, CONSTS)
            nc.gpsimd.affine_select(out=blocks, in_=blocks, compare_op=ALU.is_ge, fill=0.0, base=GROUP - 1,
                                    pattern=[[GROUP, P // GROUP], [0, GROUP]], channel_multiplier=-1
                                    ).then_inc(made, 1)

            def add(img, lo, hi):
                for t in range(lo, hi):
                    pool.wait_ge(scaled, img.at(TILES, t + 1))
                    pool.wait_ge(gain_done, img.at(TILES, t + 1))
                    dst = stage[:, t // CHUNK % 2, t % CHUNK, :]
                    nc.gpsimd.tensor_tensor(dst, dst, shiftb[:, t % 4, :], ALU.add).then_inc(added, 1)

            def products(img, prev):
                pool.wait_ge(ev["wq_copied"], img.b + 1)
                if prev:
                    pool.wait_ge(added, prev.at(TILES, 16))
                for n in range(SHARED):
                    if comes(img.at(SHARED, n - 1)):
                        pool.wait_ge(q_summed, img.at(SHARED, n - 1))
                    nc.gpsimd.tensor_tensor(shiftb[:, 2 + n % 2, :], xs[:, img.slot, DVE_DOTS + n, :], partial[:],
                                            ALU.mult).then_inc(q_product, 1)

            def gate_products(img, prev):
                pool.wait_ge(ev["v_copied"], img.b + 1)
                if prev:
                    pool.wait_ge(stored[0], prev.at(16 * CHUNKS // 2, 16 * 2))
                for n in range(GATE_SHARED):
                    nc.gpsimd.tensor_tensor(stage[:, 0, CHUNK - GATE_SHARED + n, :],
                                            xs[:, img.slot, GATE_FIRST + n, :], partial[:],
                                            ALU.mult).then_inc(t_product, 1)

            def group_power(img):
                pool.wait_ge(ev["stat_var"], img.b + 1)
                nc.gpsimd.tensor_tensor(rs[:, img.slot, :], var[:], halves[:], ALU.pow).then_inc(ev["rs"], 1)

            def layer_power(img):
                pool.wait_ge(ev["z_var"], img.b + 1)
                nc.gpsimd.tensor_tensor(zrstd[:], zvar[:], halves[:, 0:1], ALU.pow).then_inc(ev["z_rstd"], 1)

            def phase(prev, cur, nxt):
                if prev:
                    add(prev, 8, 16)
                products(cur, prev)
                if prev:
                    add(prev, 16, 23)
                layer_power(cur)
                if prev:
                    add(prev, 23, 32)
                gate_products(cur, prev)
                add(cur, 0, 5)
                if nxt:
                    group_power(nxt)
                add(cur, 5, 8)

            group_power(image(0, 0))
            phases(pool, phase)
            add(LAST, 8, 32)

        @block.scalar
        def _(act):
            def gains(img, lo, hi):
                for t in range(lo, hi):
                    s = gate[:, img.slot, t:t + 1]
                    if t % CHUNK == 0:
                        act.wait_ge(gate_done, img.at(CHUNKS, t // CHUNK + 1))
                    if comes(img.at(TILES, t - 3)):
                        act.wait_ge(added, img.at(TILES, t - 3))
                    nc.scalar.activation(shiftb[:, t % 4, :], w_row[:, img.slot, :], ACT.Copy, scale=s)
                    if comes(img.at(TILES, t - 1)):
                        act.wait_ge(scaled, img.at(TILES, t - 1))
                    nc.scalar.activation(gain_ps[t % 2][:], u_row[:, img.slot, :], ACT.Identity, scale=s,
                                         bias=1.0).then_inc(gain_done, 1)

            def product_sums(img, lo, hi):
                for n in range(lo, hi):
                    act.wait_ge(q_product, img.at(SHARED, n + 1))
                    part = shiftb[:, 2 + n % 2, :]
                    nc.scalar.activation(part, part, ACT.Copy, accum_out=qdot[:, DVE_DOTS + n:DVE_DOTS + n + 1]
                                         ).then_inc(q_summed, 1)

            def probs(cur, h):
                act.wait_ge(ev["max_neg"], cur.at(2, h + 1))
                c = slice(PARTS[h], PARTS[h + 1])
                nc.scalar.activation(prob[:, c], logit[:, c], ACT.Exp, bias=neg_max[:, h:h + 1],
                                     accum_out=mass[:, h:h + 1]).then_inc(ev["probs"], 1)

            def sums_out(cur, h):
                act.wait_ge(ev["weighted_ps"], cur.at(2, h + 1))
                nc.scalar.activation(part_sums[h], part_ps[h][:], ACT.Copy).then_inc(ev["weighted"], 1)

            def gate_product_sums(img):
                for n in range(GATE_SHARED):
                    act.wait_ge(t_product, img.at(GATE_SHARED, n + 1))
                    part = stage[:, 0, CHUNK - GATE_SHARED + n, :]
                    nc.scalar.activation(part, part, ACT.Copy, accum_out=tdot[:, GATE_FIRST + n:GATE_FIRST + n + 1]
                                         ).then_inc(t_summed, 1)

            def gate_exps(img, k):
                act.wait_ge(t_dotted, img.at(TILES - GATE_SHARED, dve_gate_dots((k + 1) * CHUNK)))
                if k == GATE_FIRST // CHUNK:
                    act.wait_ge(t_summed, img.at(GATE_SHARED, GATE_SHARED))
                c = slice(k * CHUNK, (k + 1) * CHUNK)
                nc.scalar.activation(texp[:, c], tdot[:, c], ACT.Exp, scale=-1.0, bias=shift[:]
                                     ).then_inc(gate_exp, 1)

            def stats(img):
                act.wait_ge(ev["stat_ps"], img.b + 1)
                nc.scalar.activation(partial[:], sum_ps[:], ACT.Copy).then_inc(ev["sum_copied"], 1)

            def phase(prev, cur, nxt):
                if prev:
                    gate_exps(prev, 2)
                    gains(prev, 8, 9)
                act.wait_ge(ev["wq_row"], cur.b + 1)
                nc.scalar.activation(partial[:], wq_ps[:], ACT.Copy).then_inc(ev["wq_copied"], 1)
                if prev:
                    gains(prev, 9, 18)
                product_sums(cur, 0, 3)
                probs(cur, 0)
                product_sums(cur, 3, SHARED)
                sums_out(cur, 0)
                probs(cur, 1)
                act.wait_ge(ev["max_lower"], cur.b + 1)
                nc.scalar.activation(factor[:], neg_max[:], ACT.Exp, scale=-1.0, bias=neg_all[:]
                                     ).then_inc(ev["factor"], 1)
                if prev:
                    act.wait_ge(q_summed, cur.at(SHARED, SHARED))
                    gains(prev, 18, 20)
                sums_out(cur, 1)
                if prev:
                    gains(prev, 20, 22)
                act.wait_ge(ev["z_row_ps"], cur.b + 1)
                nc.scalar.activation(partial[:], weighted_ps[:], ACT.Copy).then_inc(ev["z_row"], 1)
                if prev:
                    gains(prev, 22, 24)
                    gate_exps(prev, 3)
                    gains(prev, 24, 26)
                act.wait_ge(ev["z_beta"], cur.b + 1)
                nc.scalar.activation(zexp[:], zbet[:], ACT.Exp, scale=-1.0).then_inc(ev["z_exp"], 1)
                if prev:
                    gains(prev, 26, 28)
                act.wait_ge(ev["q_max"], cur.b + 1)
                nc.scalar.activation(qrow[:], qrow[:], ACT.Exp, bias=qmax[:], accum_out=asum[:]
                                     ).then_inc(ev["q_exp"], 1)
                act.wait_ge(ev["u_ps"], cur.b + 1)
                nc.scalar.activation(u_row[:, cur.slot, :], weighted_ps[:], ACT.Copy).then_inc(ev["u_row"], 1)
                act.wait_ge(ev["w_ps"], cur.b + 1)
                nc.scalar.activation(w_row[:, cur.slot, :], wq_ps[:], ACT.Copy).then_inc(ev["w_row"], 1)
                if prev:
                    gains(prev, 28, 32)
                act.wait_ge(ev["v_row"], cur.b + 1)
                nc.scalar.activation(partial[:], v_ps[:], ACT.Copy).then_inc(ev["v_copied"], 1)
                act.wait_ge(ev["shift"], cur.b + 1)
                gate_exps(cur, 0)
                gate_product_sums(cur)
                gains(cur, 0, 2)
                gate_exps(cur, 1)
                gains(cur, 2, 5)
                if nxt:
                    stats(nxt)
                gains(cur, 5, 8)

            stats(image(0, 0))
            phases(act, phase)
            gate_exps(LAST, 2)
            gains(LAST, 8, 15)
            gate_exps(LAST, 3)
            gains(LAST, 15, 32)

        @block.tensor
        def _(pe):
            pe.wait_ge(made, CONSTS + 1)

            def gram(img, lo, hi, sides=1):
                block = P // sides
                for t in range(lo, hi):
                    if t % QUAD == 0:
                        pe.wait_ge(loaded[img.slot][t // QUAD], img.use * 16 + 16)
                    if t == 0:
                        if comes(img.at(1, 0)):
                            pe.wait_ge(ev["square_col"], img.at(1, 0))
                        if comes(img.at(1, 0)):
                            pe.wait_ge(ev["sum_copied"], img.at(1, 0))
                    tile = xs[:, img.slot, t, :]
                    s = (t % STRIPS) * SW
                    nc.tensor.matmul(sum_ps[s:s + SW, :], ones[:, 0:SW], tile, start=t < STRIPS,
                                     stop=t >= TILES - STRIPS)
                    for j in range(J):
                        for e in range(sides):
                            lo_c = j * P + e * block
                            cols = tile[:, lo_c:lo_c + block]
                            last = nc.tensor.matmul(gram_ps[e * block:(e + 1) * block, lo_c:lo_c + block], cols, cols,
                                                    start=t == 0 and j == 0, stop=t == TILES - 1 and j == J - 1,
                                                    skip_group_check=True)
                    if t == TILES - 1:
                        last.then_inc(ev["stat_ps"], 1)

            def row(dst, column_diag):
                return nc.tensor.matmul(dst[:], ones[:], column_diag.rearrange("p j c -> p (j c)"),
                                        start=True, stop=True)

            def pool_part(cur, h):
                pe.wait_ge(ev["weighted"], cur.at(2, h + 1))
                for j in range(J):
                    last = nc.tensor.matmul(part_ps[h][:, j:j + 1], part_sums[h][:, j * P:(j + 1) * P],
                                            sel[:, 1:2], start=True, stop=True)
                last.then_inc(ev["pooled_ps"], 1)

            def stats(img):
                pe.wait_ge(ev["sum_copied"], img.b + 1)
                for j in range(J):
                    last = nc.tensor.matmul(small[:, j:j + 1], partial[:, j * P:(j + 1) * P], sel[:, 0:1],
                                            start=True, stop=True)
                last.then_inc(ev["stat_group_ps"], 1)
                pe.wait_ge(ev["stat_mean"], img.b + 1)
                pe.wait_ge(ev["square_col"], img.b + 1)
                nc.tensor.matmul(small[:, 8:8 + 2 * J], block16[:], stat[:, img.slot, :], start=True,
                                        stop=True).then_inc(ev["stat_group"], 1)
                pe.wait_ge(ev["mwq_col"], img.b + 1)
                nc.tensor.matmul(small[:, 16:17], ones[:], mwq_sum[:], start=True, stop=True)
                pe.wait_ge(ev["wq_diag"], img.b + 1)
                row(wq_ps, diag[:]).then_inc(ev["wq_row"], 1)

            def softmax(cur, h, fill):
                pe.wait_ge(ev["logits_max"], cur.at(2, h + 1))
                nc.tensor.transpose(small[0:1, P:2 * P], lmax[:, h:h + 1], ident[:]).then_inc(ev["max_t"], 1)
                if h == 0:
                    fill(11, 12)
                pe.wait_ge(ev["max_one"], cur.at(2, h + 1))
                nc.tensor.matmul(small[:, 60:61], neg_row[:], one_max[:], start=True, stop=True
                                 ).then_inc(ev["max_ps"], 1)
                if h == 0:
                    fill(12, 13)
                else:
                    pool_part(cur, 0)
                pe.wait_ge(ev["probs"], cur.at(2, h + 1))
                if h == 1:
                    nc.tensor.matmul(small[:, 62:64], ones[:], mass[:], start=True, stop=True
                                     ).then_inc(ev["mass_ps"], 1)
                lo, hi = PARTS[h], PARTS[h + 1]
                for t in range(lo, hi):
                    s = (t % STRIPS) * SW
                    last = nc.tensor.matmul(part_ps[h][s:s + SW, :], prob[:, t:t + 1].to_broadcast([P, SW]),
                                            xs[:, cur.slot, t, :], start=t < lo + STRIPS, stop=t >= hi - STRIPS)
                last.then_inc(ev["weighted_ps"], 1)

            def columns(dst, weight, rhs, blocks, depth):
                for o in range(blocks):
                    for i in range(depth):
                        last = nc.tensor.matmul(dst[:, o:o + 1], weight[:, i, o * P:(o + 1) * P], rhs[:, i:i + 1],
                                                start=i == 0, stop=i == depth - 1)
                return last

            def channel(cur, fill):
                fill(14, 15)
                pool_part(cur, 1)
                pe.wait_ge(ev["pooled"], cur.b + 1)
                for i in range(J):
                    last = nc.tensor.matmul(weighted_ps[i * SW:(i + 1) * SW, :],
                                            pool_y[:, i:i + 1].to_broadcast([P, SW]), wvz[:, i, :],
                                            start=True, stop=True)
                last.then_inc(ev["z_row_ps"], 1)
                fill(15, 16)
                pe.wait_ge(ev["z_row"], cur.b + 1)
                for j in range(J):
                    last = nc.tensor.matmul(small[:, 28 + j:29 + j], partial[:, j * P:(j + 1) * P], sel[:, 1:2],
                                            start=True, stop=True)
                last.then_inc(ev["z_ps"], 1)
                pe.wait_ge(ev["z_sq"], cur.b + 1)
                nc.tensor.matmul(small[:, 36:37], ones[:], zsq[:], start=True, stop=True
                                 ).then_inc(ev["z_var_ps"], 1)
                fill(16, 18)

            def spatial(cur, fill):
                pe.wait_ge(ev["y_mean"], cur.b + 1)
                for j in range(J):
                    last = nc.tensor.matmul(small[0:1, D:2 * D], ymean[:, j:j + 1], wq2[:, j, :], start=j == 0,
                                            stop=j == J - 1)
                last.then_inc(ev["q_ps"], 1)
                pe.wait_ge(ev["u_diag"], cur.b + 1)
                row(weighted_ps, diag[:]).then_inc(ev["u_ps"], 1)
                pe.wait_ge(ev["w_diag"], cur.b + 1)
                row(wq_ps, w_diag).then_inc(ev["w_ps"], 1)
                pe.wait_ge(ev["q_inv"], cur.b + 1)
                for h in range(H):
                    last = nc.tensor.matmul(small[:, 40 + h:41 + h], qrow[:, h * P:(h + 1) * P], ainv[:],
                                            start=True, stop=True)
                last.then_inc(ev["a_ps"], 1)
                pe.wait_ge(ev["a"], cur.b + 1)
                for h in range(H):
                    nc.tensor.matmul(v_ps[:], acol[:, h:h + 1].to_broadcast([P, P]), wv2t[:, h, :], start=h == 0,
                                     stop=h == H - 1)
                for h in range(H):
                    last = nc.tensor.matmul(small[:, 48:49], acol[:, h:h + 1].to_broadcast([P, P]),
                                            bv2_col[:, h:h + 1], start=h == 0, stop=h == H - 1)
                last.then_inc(ev["k_ps"], 1)

            def phase(prev, cur, nxt):
                def fill(lo, hi):
                    if nxt:
                        gram(nxt, lo, hi)

                fill(0, 11)
                softmax(cur, 0, fill)
                fill(13, 14)
                softmax(cur, 1, fill)
                channel(cur, fill)
                spatial(cur, fill)
                fill(18, TILES)
                if nxt:
                    stats(nxt)

            gram(image(0, 0), 0, 1)
            gram(image(0, 0), 1, TILES, 2)
            stats(image(0, 0))
            pe.wait_ge(weights_in, 16 * 2)
            pe.wait_ge(vectors_in, 16 * 8)
            for j in range(J):
                if j >= 2:
                    pe.wait_ge(product, j - 1)
                for h in range(H):
                    last = nc.tensor.matmul(gain_ps[j % 2][:], wv_t[:, h, j * P:(j + 1) * P], wz[:, h, :],
                                            start=h == 0, stop=h == H - 1)
                last.then_inc(product_ps, 1)
            columns(small[:, 52:52 + J], wz, bv_col, J, H).then_inc(bias_ps, 1)
            pe.wait_ge(bias, 2)
            nc.tensor.matmul(small[:, 56:57], ones[:], bvz_sum[:], start=True, stop=True).then_inc(bias_ps, 1)
            pe.wait_ge(spatial_in, 16 * 2)
            phases(pe, phase)

        @block.vector
        def _(dve):
            v = nc.vector
            dve.wait_ge(made, CONSTS + 1)
            dve.wait_ge(vectors_in, 16 * 8)
            v.tensor_scalar(bq_part[:], bq[:], 1.0 / P, None, ALU.mult).then_inc(bq_parted, 1)
            dve.wait_ge(bq_parted, 1)

            def dots(img, lo, hi, row_ps, dst, junk, dotted, count, before):
                for t in range(lo, hi):
                    if comes(img.at(count, before(t) - 1)):
                        dve.wait_ge(dotted, img.at(count, before(t) - 1))
                    v.tensor_tensor_reduce(out=junk[:, t % 2, :], in0=xs[:, img.slot, t, :], in1=row_ps[:],
                                           scale=1.0, scalar=0.0, op0=ALU.mult, op1=ALU.add,
                                           accum_out=dst[:, t:t + 1]).then_inc(dotted, 1)

            def q_dots(img, lo, hi):
                dots(img, lo, hi, wq_ps, qdot, q_junk, q_dotted, DVE_DOTS, int)

            def gate_dots(img, lo, hi):
                dots(img, lo, hi, v_ps, tdot, t_junk, t_dotted, TILES - GATE_SHARED, dve_gate_dots)

            def gates(img, k):
                c = slice(k * CHUNK, (k + 1) * CHUNK)
                dve.wait_ge(gate_exp, img.at(CHUNKS, k + 1))
                v.tensor_scalar(tden[:, c], texp[:, c], 1.0, None, ALU.add).then_inc(gate_den, 1)
                dve.wait_ge(gate_den, img.at(CHUNKS, k + 1))
                v.reciprocal(gate[:, img.slot, c], tden[:, c]).then_inc(gate_done, 1)

            def scale(img, lo, hi):
                for t in range(lo, hi):
                    k, r = t // CHUNK, t % CHUNK
                    if r == 0:
                        if comes(img.at(16 * CHUNKS // 2, 16 * (k // 2))):
                            dve.wait_ge(stored[k % 2], img.at(16 * CHUNKS // 2, 16 * (k // 2)))
                    dve.wait_ge(gain_done, img.at(TILES, t + 1))
                    v.tensor_tensor(stage[:, k % 2, r, :], xs[:, img.slot, t, :], gain_ps[t % 2][:],
                                    ALU.mult).then_inc(scaled, 1)

            def part_max(img, h):
                c = slice(PARTS[h], PARTS[h + 1])
                dve.wait_ge(q_dotted, img.at(DVE_DOTS, min(PARTS[h + 1], DVE_DOTS)))
                if h == 1:
                    dve.wait_ge(q_summed, img.at(SHARED, SHARED))
                v.tensor_scalar(logit[:, c], qdot[:, c], small[:, 16:17], None, ALU.add, ALU.max,
                                accum_out=lmax[:, h:h + 1]).then_inc(ev["logits_max"], 1)
                dve.wait_ge(ev["logits_max"], img.at(2, h + 1))

            def whole_max(img, h):
                dve.wait_ge(ev["max_t"], img.at(2, h + 1))
                v.tensor_reduce(one_max[:], small[0:1, P:2 * P], AX.X, ALU.max).then_inc(ev["max_one"], 1)

            def lower_max(img, h):
                dve.wait_ge(ev["max_ps"], img.at(2, h + 1))
                v.tensor_copy(neg_max[:, h:h + 1], small[:, 60:61]).then_inc(ev["max_neg"], 1)

            def diagonal(dst, column, name):
                ins = v.tensor_tensor(dst, ident[:].unsqueeze(1).to_broadcast([P, J, P]),
                                      column.unsqueeze(2).to_broadcast([P, J, P]), ALU.mult)
                ins.then_inc(ev[name], 1)

            def stats(img, cur):
                def fill(dot, tile):
                    if cur:
                        gate_dots(cur, dot[0], dot[1])
                        scale(cur, tile[0], tile[1])

                dve.wait_ge(ev["stat_ps"], img.b + 1)
                for j in range(J):
                    last = v.tensor_tensor_reduce(out=diag[:, j, :],
                                                  in0=gram_ps[:, j * P:(j + 1) * P], in1=ident[:],
                                                  scale=1.0 / TOKENS, scalar=0.0, op0=ALU.mult, op1=ALU.add,
                                                  accum_out=stat[:, img.slot, J + j:J + j + 1])
                last.then_inc(ev["square_col"], 1)
                dve.wait_ge(ev["square_col"], img.b + 1)
                fill((19, 20), (4, 5))
                dve.wait_ge(ev["stat_group_ps"], img.b + 1)
                v.tensor_copy(stat[:, img.slot, 0:J], small[:, 0:J]).then_inc(ev["stat_mean"], 1)
                fill((20, 21), (5, 5))
                dve.wait_ge(ev["stat_group"], img.b + 1)
                g = gstat[:, img.slot, :]
                v.tensor_copy(g, small[:, 8:8 + 2 * J]).then_inc(ev["stat_group_sb"], 1)
                dve.wait_ge(ev["stat_group_sb"], img.b + 1)
                v.tensor_tensor(m2[:], g[:, 0:J], g[:, 0:J], ALU.mult).then_inc(ev["stat_m2"], 1)
                dve.wait_ge(ev["stat_m2"], img.b + 1)
                v.scalar_tensor_tensor(out=var[:], in0=g[:, J:2 * J], scalar=GN_EPS, in1=m2[:], op0=ALU.add,
                                            op1=ALU.subtract).then_inc(ev["stat_var"], 1)
                dve.wait_ge(ev["stat_var"], img.b + 1)
                fill((21, 22), (5, 6))
                dve.wait_ge(ev["rs"], img.b + 1)
                v.tensor_tensor(wqs[:], wq_col[:], rs[:, img.slot, :], ALU.mult).then_inc(ev["wq_col"], 1)
                dve.wait_ge(ev["wq_col"], img.b + 1)
                diagonal(diag[:], wqs[:], "wq_diag")
                v.tensor_tensor_reduce(out=mwq[:], in0=g[:, 0:J], in1=wqs[:], scale=-1.0, scalar=bq_part[:],
                                       op0=ALU.mult, op1=ALU.add, accum_out=mwq_sum[:]
                                       ).then_inc(ev["mwq_col"], 1)
                fill((22, 24), (6, 8))

            def phase(prev, cur, nxt):
                def fill_prev(lo, hi):
                    if prev:
                        scale(prev, lo, hi)

                def dots_prev(lo, hi):
                    if prev:
                        gate_dots(prev, lo, hi)

                m = gstat[:, cur.slot, 0:J]
                r = rs[:, cur.slot, :]
                fill_prev(8, 9)
                dve.wait_ge(ev["wq_copied"], cur.b + 1)
                q_dots(cur, 0, 1)
                if prev:
                    gates(prev, 2)
                for n in range(1, 8):
                    q_dots(cur, n, n + 1)
                    fill_prev(8 + n, 9 + n)
                q_dots(cur, 8, PART)
                part_max(cur, 0)
                q_dots(cur, PART, PART + 2)
                whole_max(cur, 0)
                q_dots(cur, PART + 2, PART + 4)
                lower_max(cur, 0)
                q_dots(cur, PART + 4, DVE_DOTS)
                part_max(cur, 1)
                dots_prev(24, 25)
                whole_max(cur, 1)
                dots_prev(25, 26)
                lower_max(cur, 1)
                fill_prev(16, 17)
                dve.wait_ge(ev["max_neg"], cur.at(2, 2))
                v.tensor_tensor(neg_all[:], neg_max[:, 0:1], neg_max[:, 1:2], ALU.min
                                ).then_inc(ev["max_lower"], 1)
                dots_prev(26, 27)
                fill_prev(17, 18)
                dve.wait_ge(ev["factor"], cur.b + 1)
                dve.wait_ge(ev["mass_ps"], cur.b + 1)
                v.tensor_tensor_reduce(out=mass_junk[:], in0=small[:, 62:64], in1=factor[:], scale=1.0, scalar=0.0,
                                       op0=ALU.mult, op1=ALU.add, accum_out=mass_sum[:]
                                       ).then_inc(ev["mass_sum"], 1)
                dots_prev(27, 28)
                dve.wait_ge(ev["mass_sum"], cur.b + 1)
                v.reciprocal(inv_mass[:], mass_sum[:]).then_inc(ev["mass_inv"], 1)
                fill_prev(18, 19)
                dve.wait_ge(ev["mass_inv"], cur.b + 1)
                v.tensor_scalar(part_weight[:], factor[:], inv_mass[:], None, ALU.mult
                                ).then_inc(ev["part_weight"], 1)
                dots_prev(28, 29)
                dve.wait_ge(ev["part_weight"], cur.b + 1)
                dve.wait_ge(ev["pooled_ps"], cur.at(2, 1))
                v.scalar_tensor_tensor(out=pool_a[:], in0=part_ps[0][:, 0:J], scalar=part_weight[:, 0:1], in1=m,
                                       op0=ALU.mult, op1=ALU.subtract).then_inc(ev["pooled_a"], 1)
                fill_prev(19, 20)
                dve.wait_ge(ev["pooled_ps"], cur.at(2, 2))
                dve.wait_ge(ev["pooled_a"], cur.b + 1)
                v.scalar_tensor_tensor(out=pool_n[:], in0=part_ps[1][:, 0:J], scalar=part_weight[:, 1:2],
                                       in1=pool_a[:], op0=ALU.mult, op1=ALU.add).then_inc(ev["pooled_n"], 1)
                dve.wait_ge(ev["pooled_n"], cur.b + 1)
                v.tensor_tensor(pool_y[:], pool_n[:], r, ALU.mult).then_inc(ev["pooled"], 1)
                v.tensor_tensor(ycent[:], stat[:, cur.slot, 0:J], m, ALU.subtract).then_inc(ev["y_cent"], 1)
                dots_prev(29, 30)
                fill_prev(20, 21)
                dots_prev(30, 31)
                fill_prev(21, 22)
                dots_prev(31, 32)
                fill_prev(22, 23)
                dve.wait_ge(ev["z_ps"], cur.b + 1)
                v.tensor_tensor(zcent[:], small[:, 28:28 + J], bvz[:], ALU.add).then_inc(ev["z"], 1)
                dve.wait_ge(ev["z"], cur.b + 1)
                v.tensor_tensor_reduce(out=zjunk[:], in0=zcent[:], in1=zcent[:], scale=1.0 / C, scalar=0.0,
                                       op0=ALU.mult, op1=ALU.add, accum_out=zsq[:]).then_inc(ev["z_sq"], 1)
                v.tensor_tensor(zgam[:], zcent[:], gamma[:], ALU.mult).then_inc(ev["z_gamma"], 1)
                if prev:
                    gates(prev, 3)
                dve.wait_ge(ev["z_var_ps"], cur.b + 1)
                v.tensor_scalar(zvar[:], small[:, 36:37], LN_EPS, None, ALU.add).then_inc(ev["z_var"], 1)
                fill_prev(23, 24)
                dve.wait_ge(ev["z_gamma"], cur.b + 1)
                dve.wait_ge(ev["z_rstd"], cur.b + 1)
                v.scalar_tensor_tensor(out=zbet[:], in0=zgam[:], scalar=zrstd[:], in1=beta[:], op0=ALU.mult,
                                       op1=ALU.add).then_inc(ev["z_beta"], 1)
                fill_prev(24, 25)
                dve.wait_ge(ev["z_exp"], cur.b + 1)
                v.tensor_scalar(zden[:], zexp[:], 1.0, None, ALU.add).then_inc(ev["z_den"], 1)
                dve.wait_ge(ev["z_den"], cur.b + 1)
                v.reciprocal(cw[:], zden[:]).then_inc(ev["cw"], 1)
                dve.wait_ge(ev["cw"], cur.b + 1)
                v.tensor_tensor(ucol[:], cw[:], r, ALU.mult).then_inc(ev["u"], 1)
                dve.wait_ge(ev["u"], cur.b + 1)
                v.tensor_tensor(ymean[:], ycent[:], ucol[:], ALU.mult).then_inc(ev["y_mean"], 1)
                diagonal(diag[:], ucol[:], "u_diag")
                v.scalar_tensor_tensor(out=wcol[:], in0=ucol[:], scalar=-1.0, in1=m, op0=ALU.mult,
                                       op1=ALU.mult).then_inc(ev["w"], 1)
                fill_prev(25, 26)
                dve.wait_ge(ev["w"], cur.b + 1)
                diagonal(w_diag, wcol[:], "w_diag")
                dve.wait_ge(ev["q_ps"], cur.b + 1)
                v.tensor_tensor(qrow[:], small[0:1, D:2 * D], bq2_row[:], ALU.add).then_inc(ev["q_row"], 1)
                dve.wait_ge(ev["q_row"], cur.b + 1)
                v.tensor_reduce(qmax[:], qrow[:], AX.X, ALU.max, negate=True).then_inc(ev["q_max"], 1)
                fill_prev(26, 27)
                dve.wait_ge(ev["q_exp"], cur.b + 1)
                v.reciprocal(ainv[:], asum[:]).then_inc(ev["q_inv"], 1)
                fill_prev(27, 28)
                dve.wait_ge(ev["a_ps"], cur.b + 1)
                v.tensor_copy(acol[:], small[:, 40:40 + H]).then_inc(ev["a"], 1)
                dve.wait_ge(ev["a"], cur.b + 1)
                fill_prev(28, 30)
                dve.wait_ge(ev["k_ps"], cur.b + 1)
                v.tensor_scalar(a_bias[:], small[:, 48:49], -1.0, None, ALU.mult).then_inc(ev["a_bias"], 1)
                fill_prev(30, 31)
                dve.wait_ge(ev["a_bias"], cur.b + 1)
                dve.wait_ge(ev["w_row"], cur.b + 1)
                v.tensor_tensor_reduce(out=q_junk[:, 0, :], in0=v_ps[:], in1=w_row[:, cur.slot, :], scale=-1.0,
                                       scalar=a_bias[:], op0=ALU.mult, op1=ALU.add, accum_out=shift[:]
                                       ).then_inc(ev["shift"], 1)
                dve.wait_ge(ev["u_row"], cur.b + 1)
                v.tensor_tensor(v_ps[:], v_ps[:], u_row[:, cur.slot, :], ALU.mult).then_inc(ev["v_row"], 1)
                fill_prev(31, 32)
                dve.wait_ge(ev["v_copied"], cur.b + 1)
                gate_dots(cur, 0, GATE_FIRST)
                gates(cur, 0)
                for n in range(3):
                    gate_dots(cur, 16 + n, 17 + n)
                    scale(cur, n, 1 + n)
                gates(cur, 1)
                scale(cur, 3, 4)
                if nxt:
                    stats(nxt, cur)
                else:
                    gate_dots(cur, 19, 24)
                    scale(cur, 4, 8)

            stats(image(0, 0), None)
            for j in range(J):
                dve.wait_ge(product_ps, j + 1)
                v.tensor_reduce(wvz_sum[:, j:j + 1], gain_ps[j % 2][:], AX.X, ALU.add).then_inc(product_sum, 1)
                dve.wait_ge(product_sum, j + 1)
                v.tensor_scalar(wvz_mean[:, j:j + 1], wvz_sum[:, j:j + 1], 1.0 / C, None, ALU.mult
                                ).then_inc(product_mean, 1)
                dve.wait_ge(product_mean, j + 1)
                v.tensor_scalar(wvz[:, j, :], gain_ps[j % 2][:], wvz_mean[:, j:j + 1], None, ALU.subtract
                                ).then_inc(product, 1)
            dve.wait_ge(bias_ps, 1)
            v.tensor_tensor(bvz[:], small[:, 52:52 + J], bz_col[:], ALU.add).then_inc(bias, 1)
            dve.wait_ge(bias, 1)
            v.tensor_reduce(bvz_sum[:], bvz[:], AX.X, ALU.add).then_inc(bias, 1)
            dve.wait_ge(bias_ps, 2)
            v.tensor_scalar(bvz_mean[:], small[:, 56:57], 1.0 / C, None, ALU.mult).then_inc(bias, 1)
            dve.wait_ge(bias, 3)
            v.tensor_scalar(bvz[:], bvz[:], bvz_mean[:], None, ALU.subtract).then_inc(bias, 1)
            dve.wait_ge(bias, 4)
            phases(dve, phase)
            gate_dots(LAST, 24, 28)
            gates(LAST, 2)
            scale(LAST, 8, 10)
            gate_dots(LAST, 28, 32)
            scale(LAST, 10, 14)
            gates(LAST, 3)
            scale(LAST, 14, 32)


def kernel(**inputs):
    import numpy as np
    import concourse.bacc as bacc
    from concourse.bass_utils import run_bass_kernel_spmd as run

    nc = bacc.Bacc("TRN2", target_bir_lowering=False, num_devices=1)
    arrays = {"x": np.ascontiguousarray(inputs["x"])}
    for name in ("ch_wv_b", "ch_wq_w", "ch_wq_b", "ch_wz_w", "ch_wz_b", "ln_gamma", "ln_beta",
                 "sp_wv_b", "sp_wq_w", "sp_wq_b"):
        arrays[name] = np.ascontiguousarray(inputs[f"L0_conv_{name}"])
    for name in ("ch_wq_w", "ch_wv_b", "ch_wz_b", "ln_gamma", "ln_beta", "sp_wv_b"):
        arrays[name] = np.ascontiguousarray(np.transpose(np.reshape(arrays[name], (-1, P))))
    for name in ("ch_wv_w", "sp_wv_w"):
        arrays[f"{name}_t"] = np.ascontiguousarray(np.transpose(inputs[f"L0_conv_{name}"]))
    w = {name: nc.dram_tensor(name, a.shape, mybir.dt.from_np(a.dtype), kind="ExternalInput").ap()
         for name, a in arrays.items()}
    out = nc.dram_tensor("out", arrays["x"].shape, F32, kind="ExternalOutput").ap()
    build(nc, w["x"], w, out)
    return run(nc, [arrays], core_ids=[0]).results[0]["out"]
```
